# Optimizing a Trainium2 kernel written in Bass

```python
import numpy as np
import jax
import jax.numpy as jnp

def _softmax(x, axis=-1):
    return jax.nn.softmax(x, axis=axis)

def _gelu(x):
    return jax.nn.gelu(x, approximate=True)

def _silu(x):
    return jax.nn.silu(x)

def _sigmoid(x):
    return jax.nn.sigmoid(x)

def _layernorm(x, axis=-1, eps=1e-05):
    m = jnp.mean(x, axis=axis, keepdims=True)
    v = jnp.var(x, axis=axis, keepdims=True)
    return (x - m) / jnp.sqrt(v + eps)

def _scatter_add(tgt, idx, src, axis=0):
    return tgt.at[idx].add(src)

def _segment_sum(src, seg, n):
    return jax.ops.segment_sum(src, seg, n)
kernel_name = 'mk_gnn_resnorm_d2_gnn_r32_80f83f'

def setup_inputs(seed: int=0):
    np.random.seed(seed)
    _w = jnp.asarray

    def _rec_inputs():
        import jax
        import jax.numpy as jnp
        _gk = jax.random.key(seed)
        x = -0.0009044 + 1 * jax.random.normal(jax.random.fold_in(_gk, 1), (3125, 16), jnp.float32)
        src = jax.random.randint(jax.random.fold_in(_gk, 2), (100000,), 0, 3125, jnp.int32)
        dst = jax.random.randint(jax.random.fold_in(_gk, 3), (100000,), 0, 3125, jnp.int32)
        _o = jnp.argsort(dst, stable=True)
        src = src[_o]
        dst = dst[_o]
        edge_attr_8 = -5.3897e-05 + 0.999841 * jax.random.normal(jax.random.fold_in(_gk, 11), (100000, 8), jnp.float32)
        node_vec1 = -0.00472126 + 0.997171 * jax.random.normal(jax.random.fold_in(_gk, 13), (3125, 1), jnp.float32)
        return (x, src, dst, edge_attr_8, node_vec1)
    x, src, dst, edge_attr_8, node_vec1 = _rec_inputs()

    def _L0_gnn_setup():
        import jax, jax.numpy as jnp
        import numpy as np
        N_NODES = 3125
        N_EDGES = 100000
        D_NODE = 16
        D_EDGE = 8
        D_HIDDEN = 16
        key = jax.random.key(seed)
        ks = jax.random.split(key, 8)
        node_features = jax.random.normal(ks[0], (N_NODES, D_NODE), dtype=jnp.float32)
        edge_attr_e3nn = jax.random.normal(ks[1], (N_EDGES, D_EDGE), dtype=jnp.float32)
        node_attr_scalar_raw = jax.random.normal(ks[2], (N_NODES, 1), dtype=jnp.float32)
        W_msg_tp = jax.random.normal(ks[3], (D_NODE, D_EDGE, D_HIDDEN), dtype=jnp.float32)
        W_msg_lin = jax.random.normal(ks[4], (D_HIDDEN, D_HIDDEN), dtype=jnp.float32)
        W_upd_tp = jax.random.normal(ks[5], (D_NODE, D_HIDDEN, D_HIDDEN), dtype=jnp.float32)
        W_upd_lin = jax.random.normal(ks[6], (D_HIDDEN, D_NODE), dtype=jnp.float32)
        edge_index = jax.random.randint(ks[7], (2, N_EDGES), 0, N_NODES, dtype=jnp.int64)
        return {'node_features': node_features, 'edge_attr_e3nn': edge_attr_e3nn, 'node_attr_scalar_raw': node_attr_scalar_raw, 'W_msg_tp': W_msg_tp, 'W_msg_lin': W_msg_lin, 'W_upd_tp': W_upd_tp, 'W_upd_lin': W_upd_lin, 'edge_index': edge_index}
    _L0_gnn_all = _L0_gnn_setup()
    _L0_gnn_in = {k: v for k, v in _L0_gnn_all.items() if k in ('W_msg_tp', 'W_msg_lin', 'W_upd_tp', 'W_upd_lin')}
    del _L0_gnn_all

    def _L1_gnn_setup():
        import jax, jax.numpy as jnp
        import numpy as np
        STALK_DIM = 16
        N_NODES = 50000
        N_EDGES = 12500
        HIDDEN = 64
        key = jax.random.key(seed)
        k1, k2, k3, k4 = jax.random.split(key, 4)
        d = STALK_DIM
        x = jax.random.normal(k1, (N_NODES, d), dtype=jnp.float32)
        edge_index = jax.random.randint(k2, (2, N_EDGES), 0, N_NODES, dtype=jnp.int64)
        W1 = jax.random.normal(k3, (HIDDEN, 2 * d), dtype=jnp.float32) * (1.0 / np.sqrt(2 * d))
        b1 = jnp.zeros((HIDDEN,), dtype=jnp.float32)
        W2 = jax.random.normal(k4, (d, HIDDEN), dtype=jnp.float32) * (1.0 / np.sqrt(HIDDEN))
        b2 = jnp.zeros((d,), dtype=jnp.float32)
        return {'x': x, 'edge_index': edge_index, 'W1': W1, 'b1': b1, 'W2': W2, 'b2': b2}
    _L1_gnn_all = _L1_gnn_setup()
    _L1_gnn_in = {k: v for k, v in _L1_gnn_all.items() if k in ('W1', 'b1', 'W2', 'b2')}
    del _L1_gnn_all
    return {'x': x, 'src': src, 'dst': dst, 'edge_attr_8': edge_attr_8, 'node_vec1': node_vec1, 'L0_gnn_W_msg_tp': _L0_gnn_in['W_msg_tp'], 'L0_gnn_W_msg_lin': _L0_gnn_in['W_msg_lin'], 'L0_gnn_W_upd_tp': _L0_gnn_in['W_upd_tp'], 'L0_gnn_W_upd_lin': _L0_gnn_in['W_upd_lin'], 'L1_gnn_W1': _L1_gnn_in['W1'], 'L1_gnn_b1': _L1_gnn_in['b1'], 'L1_gnn_W2': _L1_gnn_in['W2'], 'L1_gnn_b2': _L1_gnn_in['b2']}

def reference(x, src, dst, edge_attr_8, node_vec1, L0_gnn_W_msg_tp, L0_gnn_W_msg_lin, L0_gnn_W_upd_tp, L0_gnn_W_upd_lin, L1_gnn_W1, L1_gnn_b1, L1_gnn_W2, L1_gnn_b2):
    import jax
    import jax.numpy as jnp

    def _L0_gnn_ref(node_features, edge_attr_e3nn, node_attr_scalar_raw, W_msg_tp, W_msg_lin, W_upd_tp, W_upd_lin, edge_index):
        import jax, jax.numpy as jnp
        import numpy as np
        N_NODES = 3125
        N_EDGES = 100000
        D_NODE = 16
        D_EDGE = 8
        D_HIDDEN = 16
        n_nodes = node_features.shape[0]
        row = edge_index[0]
        col = edge_index[1]
        norm_msg_tp = 1.0 / np.float32(np.sqrt(D_NODE * D_EDGE))
        norm_upd_tp = 1.0 / np.float32(np.sqrt(D_NODE * D_HIDDEN))
        norm_lin = 1.0 / np.float32(np.sqrt(D_HIDDEN))
        x_j = node_features[col]
        m = jnp.einsum('ei,ej,ijh->eh', x_j, edge_attr_e3nn, W_msg_tp) * norm_msg_tp
        m = jax.nn.silu(m)
        m = m @ W_msg_lin * norm_lin
        agg = jax.ops.segment_sum(m, row, num_segments=n_nodes)
        u = jnp.einsum('ni,nh,ihk->nk', node_features, agg, W_upd_tp) * norm_upd_tp
        u = jax.nn.silu(u)
        u = u @ W_upd_lin * norm_lin
        return node_features + u

    def _L1_gnn_ref(x, edge_index, W1, b1, W2, b2):
        import jax, jax.numpy as jnp
        import numpy as np
        STALK_DIM = 16
        N_NODES = 50000
        N_EDGES = 12500
        HIDDEN = 64
        d = x.shape[1]
        n = x.shape[0]
        src, dst = (edge_index[0], edge_index[1])
        xs, xd = (x[src], x[dst])

        def reflection(a, b):
            h = jax.nn.relu(jnp.concatenate([a, b], axis=1) @ W1.T + b1)
            return h @ W2.T + b2

        def householder(v):
            vn = v / jnp.maximum(jnp.linalg.norm(v, axis=1, keepdims=True), 1e-12)
            return jnp.eye(d, dtype=v.dtype)[None] - 2.0 * vn[:, :, None] * vn[:, None, :]
        F_s = householder(reflection(xs, xd))
        F_d = householder(reflection(xd, xs))
        L_sd = -jnp.einsum('eki,ekj->eij', F_s, F_d)
        ones_e = jnp.ones(src.shape[0], dtype=x.dtype)
        deg = jnp.zeros(n, dtype=x.dtype).at[src].add(ones_e).at[dst].add(ones_e)
        deg_inv_sqrt = 1.0 / jnp.sqrt(jnp.maximum(deg, 1e-05))
        coef = deg_inv_sqrt[src] * deg_inv_sqrt[dst]
        msg_s = coef[:, None] * jnp.einsum('eij,ej->ei', L_sd, xd)
        msg_d = coef[:, None] * jnp.einsum('eji,ej->ei', L_sd, xs)
        out = x - jnp.zeros_like(x).at[src].add(msg_s) - jnp.zeros_like(x).at[dst].add(msg_d)
        return jax.nn.relu(out)
    edge_index = jnp.stack([src, dst])
    x = _layernorm(x + _L0_gnn_ref(x, edge_attr_8, node_vec1, L0_gnn_W_msg_tp, L0_gnn_W_msg_lin, L0_gnn_W_upd_tp, L0_gnn_W_upd_lin, edge_index), axis=-1)
    x = _layernorm(x + _L1_gnn_ref(x, edge_index, L1_gnn_W1, L1_gnn_b1, L1_gnn_W2, L1_gnn_b2), axis=-1)
    return x

_drawn_inputs = setup_inputs


def setup_inputs(seed=0):
    import zlib

    import numpy as np

    out = dict(_drawn_inputs(seed))
    spreads = {'L1_gnn_b1': (0.0, 0.756), 'L1_gnn_b2': (0.0, 0.8)}
    factors = {}
    for name, (base, spread) in spreads.items():
        noise = np.random.default_rng([zlib.crc32(name.encode()), seed]).standard_normal(out[name].shape)
        drawn = base * np.exp(spread * noise) if base else spread * noise
        out[name] = jnp.asarray(drawn.astype(out[name].dtype))
    for name, factor in factors.items():
        out[name] = (out[name] * factor).astype(out[name].dtype)
    return out
```

```python
from contextlib import ExitStack

import concourse.bass as bass
from concourse import mybir

ALU = mybir.AluOpType
ACT = mybir.ActivationFunctionType
F32 = mybir.dt.float32
BF16 = mybir.dt.bfloat16
I16 = mybir.dt.int16
I32 = mybir.dt.int32
AX = mybir.AxisListType.X

EP = 125
CH = 16
Q = 4
QC = CH // Q
P = 128
NB = 5
NA = 5
BLOCKS = NA * NB
PADB = 32
PARTS = 3
NORM_EPS = 1e-5
DEG_FLOOR = 1e-5
UNIT_FLOOR = 1e-12


def bcast(ap, shape):
    return ap.broadcast_to(list(shape))


class Chain:

    def __init__(self, eng, sem, per_step=0):
        self.eng, self.sem, self.per, self.base, self.k = eng, sem, per_step, 0, 0

    def step(self, s):
        assert self.k in (0, self.per)
        self.base, self.k = s * self.per, 0

    def link(self, ins):
        self.k += 1
        ins.then_inc(self.sem, 1)
        self.eng.wait_ge(self.sem, self.base + self.k)


def run_tiles(eng, tiles, front, back):
    for s in range(3):
        front(s, s % 2)
        if s:
            back(s - 1, (s - 1) % 2)
    with eng.Fori(3, tiles - 2, 2) as i:
        front(i, 1)
        back(i - 1, 0)
        front(i + 1, 0)
        back(i, 1)
    front(tiles - 1, 1)
    back(tiles - 2, 0)
    back(tiles - 1, 1)


def landed(s, k, dmas):
    return s * (8 * dmas) + (16 - 8 * k) * dmas


def early(s, n):
    return isinstance(s, int) and s < n


def gnn_resnorm_kernel(nc, x, src, dst, edge_attr, w_msg_tp, w_msg_lin, w_upd_tp, w_upd_lin,
                       w1_t, b1, w2_t, b2, out):
    N, D = x.shape
    E = src.shape[0]
    DE = edge_attr.shape[1]
    HID = b1.shape[0]
    S = E // (EP * CH)
    C = S * CH
    FULLB, TAIL = N // P, N % P
    KM = D * DE
    MW = PARTS * D + 1
    GW = NA * MW
    YW = PARTS * D
    YG = NA * YW
    NT = NB * P
    assert S * EP * CH == E and S % 2 == 0 and KM == P and BLOCKS * P >= N and 2 * HID == P

    with ExitStack() as ctx:
        def sb(name, shape, dt=F32):
            return ctx.enter_context(nc.sbuf_tensor(name, shape, dt))

        def ps(name, shape):
            return ctx.enter_context(nc.psum_tensor(name, shape, F32))

        def sem(name):
            return ctx.enter_context(nc.semaphore(name))

        table_s = nc.dram_tensor("table_s", (BLOCKS * P, 2 * D), F32, kind="Internal").ap()
        table_d = nc.dram_tensor("table_d", (BLOCKS * P, 2 * D), F32, kind="Internal").ap()

        acc = ps("acc", [P, 3, 512])
        tp = ps("tp", [P, 2, 512])
        mm = ps("mm", [P, 2, 512])
        vv = ps("vv", [P, 512])

        iota_n = sb("iota_n", [P, NT], I16)
        iota_p = sb("iota_p", [P, 1], I32)
        part_id = sb("part_id", [P, 1])
        ident = sb("ident", [P, P])
        zeros = sb("zeros", [P, 512], BF16)
        w_msg = sb("w_msg", [P, D])
        w_upd = sb("w_upd", [P, 2, D])
        bd_msg = sb("bd_msg", [P, P])
        bd_upd = sb("bd_upd", [P, P])
        w1 = sb("w1", [2 * D, 2 * HID])
        w2 = sb("w2", [2 * HID, 2 * D])
        bias1 = sb("bias1", [2 * HID, 1])
        bias2 = sb("bias2", [EP, 2, D])
        idx = [sb("src_idx", [EP, C], I32), sb("dst_idx", [EP, C], I32)]
        idx_now = sb("idx_now", [EP, 2, 2, CH], I32)
        fidx = sb("fidx", [EP, C])
        span = sb("span", [EP, C])
        within = [sb("src_within", [EP, C]), sb("dst_within", [EP, C])]
        in_span = [sb("src_in_span", [EP, C, NA], BF16), sb("dst_in_span", [EP, C, NA], BF16)]
        xn = sb("xn", [P, BLOCKS, D])
        sums = sb("sums", [P, 3, 512])
        agg = sb("agg", [P, PADB, D])
        aggl = sb("aggl", [P, PADB, D])
        deg = sb("deg", [P, BLOCKS])
        dis = sb("dis", [P, BLOCKS])
        tmp = sb("tmp", [P, BLOCKS, D])
        tmp2 = sb("tmp2", [P, BLOCKS, D])
        stat = sb("stat", [P, BLOCKS])
        root = sb("root", [P, BLOCKS])
        inv = sb("inv", [P, BLOCKS])
        newton = sb("newton", [P, BLOCKS])
        x1 = sb("x1", [P, BLOCKS, D])
        xz = sb("xz", [P, BLOCKS, 3 * D])
        nouter = sb("nouter", [P, BLOCKS, D, D])
        turned = sb("turned", [P, 2, 512])
        attr = sb("attr", [EP, 2, CH, DE])
        xj = sb("xj", [EP, 2, CH, D])
        outer = sb("outer", [EP, 2, CH, D, DE])
        outer_t = sb("outer_t", [P, 2, 512])
        msg = sb("msg", [EP, 2, CH, 2, D])
        rest = sb("rest", [EP, CH, 2, D])
        parts = sb("parts", [EP, CH, MW], BF16)
        parts2 = sb("parts2", [EP, 2, CH, YW], BF16)
        prod = sb("prod", [EP, 2, CH, NA, MW], BF16)
        prod2 = sb("prod2", [EP, 2, 2, CH, NA, YW], BF16)
        hot = sb("hot", [EP, 4, NT], BF16)
        dhot = sb("dhot", [EP, 4, NT], BF16)
        gath = sb("gath", [EP, 2, CH, 4, D])
        x_t = sb("x_t", [2 * D, 2, 512])
        h = sb("h", [P, 2, 512])
        v = sb("v", [EP, CH, 2, D])
        sq = sb("sq", [EP, CH, 2, D])
        t1 = sb("t1", [EP, CH, 2, D])
        scal = sb("scal", [EP, CH, 2])
        rnorm = sb("rnorm", [EP, CH, 2])

        idx_in = sem("idx_in")
        nodes_in = sem("nodes_in")
        weights_in = sem("weights_in")
        iota_made = sem("iota_made")
        setup = sem("setup")
        indices_ready = sem("indices_ready")
        consts_ready = sem("consts_ready")
        root_asked = sem("root_asked")
        root_given = sem("root_given")
        pool_held = sem("pool_held")
        idx_placed = sem("idx_placed")
        idx2_placed = sem("idx2_placed")
        attr_in = [sem("attr_in0"), sem("attr_in1")]
        rows_in = [sem("rows_in0"), sem("rows_in1")]
        outer_made = sem("outer_made")
        turned_pe = sem("turned_pe")
        turned_out = sem("turned_out")
        msg_pe = sem("msg_pe")
        msg_made = sem("msg_made")
        part_made = sem("part_made")
        split_chain = sem("split_chain")
        prod_made = sem("prod_made")
        hot_made = sem("hot_made")
        dhot_made = sem("dhot_made")
        hot_used = sem("hot_used")
        prod_used = sem("prod_used")
        acc_zero = sem("acc_zero")
        acc_done = sem("acc_done")
        sums_out = sem("sums_out")
        node_pe = sem("node_pe")
        node_act = sem("node_act")
        node_dve = sem("node_dve")
        node_chain = sem("node_chain")
        table_ready = sem("table_ready")
        table_out = sem("table_out")
        rows2_in = [sem("rows2_in0"), sem("rows2_in1")]
        xt_pe = sem("xt_pe")
        xt_out = sem("xt_out")
        h_pe = sem("h_pe")
        h_out = sem("h_out")
        v_pe = sem("v_pe")
        v_out = sem("v_out")
        msg2_made = sem("msg2_made")
        house_chain = sem("house_chain")
        split2_chain = sem("split2_chain")
        prod2_made = sem("prod2_made")
        hot2_made = sem("hot2_made")
        hot2_used = sem("hot2_used")
        prod2_used = sem("prod2_used")
        acc2_zero = sem("acc2_zero")
        acc2_done = sem("acc2_done")
        sums2_out = sem("sums2_out")
        out_ready = sem("out_ready")
        out_stored = sem("out_stored")

        def by_tile(ap):
            return ap.rearrange("(s p c) -> p s c", s=S, p=EP)

        attr_tiles = edge_attr.rearrange("(s p c) j -> s p (c j)", s=S, p=EP)
        x_lo = x[0:FULLB * P, :].rearrange("(h p) d -> p h d", p=P)
        out_lo = out[0:FULLB * P, :].rearrange("(h p) d -> p h d", p=P)
        N_WEIGHT_DMAS = 2 + 16 + 3 + 2 + 2 + 2

        block = ctx.enter_context(nc.Block())

        @block.sync
        def _(sp):
            for t, ap in ((0, src), (1, dst)):
                sp.dma_start(idx[t][:].rearrange("p (s c) -> p s c", c=CH), by_tile(ap)).then_inc(idx_in, 16)

            def load_attr(s, k):
                sp.dma_start(attr[:, k].rearrange("p c j -> p (c j)"),
                             attr_tiles[bass.ds(s, 1)].rearrange("o p f -> (o p) f")).then_inc(attr_in[k], 16)

            load_attr(0, 0)
            load_attr(1, 1)
            sp.wait_ge(consts_ready, 1)
            sp.dma_start(xn[:, 0:FULLB, :], x_lo).then_inc(nodes_in, 16)
            sp.dma_start(xn[0:TAIL, FULLB, :], x[FULLB * P:N, :]).then_inc(nodes_in, 16)
            sp.dma_start(w_msg[:], w_msg_tp.rearrange("i j h -> (i j) h")).then_inc(weights_in, 16)
            sp.dma_start(w_upd[:], w_upd_tp.rearrange("(t i) h k -> (i h) t k", t=2)).then_inc(weights_in, 16)
            for g in range(8):
                r = slice(g * D, (g + 1) * D)
                sp.dma_start(bd_msg[r, r], w_msg_lin).then_inc(weights_in, 16)
                sp.dma_start(bd_upd[r, r], w_upd_lin).then_inc(weights_in, 16)
            sp.dma_start(w1[:, 0:HID], w1_t).then_inc(weights_in, 16)
            sp.dma_start(w1[0:D, HID:2 * HID], w1_t[D:2 * D, :]).then_inc(weights_in, 16)
            sp.dma_start(w1[D:2 * D, HID:2 * HID], w1_t[0:D, :]).then_inc(weights_in, 16)
            for g in range(2):
                sp.dma_start(w2[g * HID:(g + 1) * HID, g * D:(g + 1) * D], w2_t).then_inc(weights_in, 16)
                sp.dma_start(bias1[g * HID:(g + 1) * HID, :], b1.unsqueeze(1)).then_inc(weights_in, 16)
                sp.dma_start(bias2[:, g, :], bcast(b2.unsqueeze(0), (EP, D))).then_inc(weights_in, 16)
            with sp.Fori(2, S - 1, 2) as i:
                for k in range(2):
                    sp.wait_ge(outer_made, i + k - 1)
                    load_attr(i + k, k)
            sp.wait_ge(table_ready, 1)
            sp.dma_start(table_s.rearrange("(h p) f -> p h f", p=P), xz[:, :, 0:2 * D]).then_inc(table_out, 16)
            sp.dma_start(table_d.rearrange("(h p) f -> p h f", p=P), xz[:, :, D:3 * D]).then_inc(table_out, 16)
            sp.wait_ge(out_ready, 1)
            sp.dma_start(out_lo, tmp[:, 0:FULLB, :]).then_inc(out_stored, 16)
            sp.dma_start(out[FULLB * P:N, :], tmp[0:TAIL, FULLB, :]).then_inc(out_stored, 16)
            sp.wait_ge(out_stored, 32)

        @block.gpsimd
        def _(pool):
            nc.gpsimd.iota(iota_n[:], [[1, NT]], base=0, channel_multiplier=0).then_inc(iota_made, 1)
            nc.gpsimd.iota(iota_p[:], [[0, 1]], base=0, channel_multiplier=1).then_inc(iota_made, 1)
            pool.wait_ge(idx_in, 32)

            def hold(signal, count):
                pool.wait_ge(signal, count)
                pool.sem_inc(pool_held, 1)

            def gather(rows, table, which, k, c, signal):
                nc.gpsimd.indirect_dma_start(
                    rows, None, table, bass.IndirectOffsetOnAxis(ap=idx_now[:, k, which, c:c + 1], axis=0)
                ).then_inc(signal, 16)

            def place_indices(which, s, k, copied, count):
                nc.gpsimd.tensor_copy(idx_now[:, k, which, :],
                                      idx[which][:, bass.ds(s * CH, CH)]).then_inc(copied, 1)
                hold(copied, count)

            def first_rows(s, k):
                if not early(s, 2):
                    hold(outer_made, s - 1)
                place_indices(1, s, k, idx_placed, s + 1)
                for c in range(CH):
                    gather(xj[:, k, c, :], x, 1, k, c, rows_in[k])

            first_rows(0, 0)
            first_rows(1, 1)
            with pool.Fori(2, S - 1, 2) as i:
                first_rows(i, 0)
                first_rows(i + 1, 1)

            pool.wait_ge(table_out, 32)

            def second_rows(s, k):
                if not early(s, 2):
                    hold(msg2_made, s - 1)
                place_indices(0, s, k, idx2_placed, s * 2 + 1)
                place_indices(1, s, k, idx2_placed, s * 2 + 2)
                for c in range(CH):
                    gather(gath[:, k, c, 0:2, :].rearrange("p a d -> p (a d)"), table_s, 0, k, c, rows2_in[k])
                    gather(gath[:, k, c, 2:4, :].rearrange("p a d -> p (a d)"), table_d, 1, k, c, rows2_in[k])

            second_rows(0, 0)
            second_rows(1, 1)
            with pool.Fori(2, S - 1, 2) as i:
                second_rows(i, 0)
                second_rows(i + 1, 1)

        @block.tensor
        def _(pe):
            T = nc.tensor

            def clear_acc(done):
                for bank in range(3):
                    ins = T.matmul(acc[:, bank, :], zeros[:, 0:P], zeros[:], start=True, stop=False,
                                   skip_group_check=True)
                ins.then_inc(done, 1)

            pe.wait_ge(consts_ready, 1)
            clear_acc(acc_zero)
            pe.wait_ge(weights_in, 16 * N_WEIGHT_DMAS)

            def front(s, k):
                pe.wait_ge(outer_made, s + 1)
                for q in range(Q):
                    if not (early(s, 1) and q < 2):
                        pe.wait_ge(turned_out, s * Q + q - 1)
                    for j in range(QC):
                        ins = T.transpose(tp[:, q % 2, j * EP:(j + 1) * EP],
                                          outer[:, k, q * QC + j].rearrange("p i j -> p (i j)"), ident[0:EP, 0:EP])
                    ins.then_inc(turned_pe, 1)
                    if q >= 1:
                        messages(s, k, q - 1)
                messages(s, k, Q - 1)

            def messages(s, k, q):
                pe.wait_ge(turned_out, s * Q + q + 1)
                if q == 0 and not early(s, 2):
                    pe.wait_ge(msg_made, s - 1)
                for j in range(QC):
                    c = q * QC + j
                    ins = T.matmul(mm[0:EP, k, c * D:(c + 1) * D], outer_t[:, q % 2, j * EP:(j + 1) * EP],
                                   w_msg[:], start=True, stop=True)
                ins.then_inc(msg_pe, 1)

            def back(s, k):
                pe.wait_ge(prod_made, s + 1)
                for c in range(CH):
                    pe.wait_ge(hot_made, s * CH + c + 1)
                    for b in range(NB):
                        ins = T.matmul(acc[:, b // 2, (b % 2) * GW:(b % 2) * GW + GW],
                                       hot[:, c % 4, b * P:(b + 1) * P],
                                       prod[:, k, c].rearrange("p a m -> p (a m)"),
                                       start=False, stop=False, skip_group_check=True)
                    for b in range(NB):
                        ins = T.matmul(acc[:, 2, GW + b * NA:GW + (b + 1) * NA],
                                       dhot[:, c % 4, b * P:(b + 1) * P],
                                       in_span[1][:, bass.ds(s * CH + c, 1), :].rearrange("p o a -> p (o a)"),
                                       start=False, stop=False, skip_group_check=True)
                    ins.then_inc(hot_used, 1)

            run_tiles(pe, S, front, back)
            T.matmul(vv[0:2, 0:2], zeros[:, 0:2], zeros[:, 0:2], start=True, stop=True).then_inc(acc_done, 1)

            def turn_and_apply(source, weights, ready, first):
                pe.wait_ge(node_dve, ready)
                for g in range(4):
                    ins = T.transpose(tp[:, 0, g * P:(g + 1) * P],
                                      source[:, g * 8:(g + 1) * 8, :].rearrange("p g d -> p (g d)"), ident[:])
                ins.then_inc(node_pe, 1)
                pe.wait_ge(node_act, first)
                for g in range(4):
                    ins = T.matmul(mm[:, 0, g * P:(g + 1) * P], turned[:, 0, g * P:(g + 1) * P], weights[:],
                                   start=True, stop=True)
                ins.then_inc(node_pe, 1)

            turn_and_apply(agg, bd_msg, 1, 1)
            pe.wait_ge(node_dve, 2)
            steps = (BLOCKS + 1) // 2

            def upd_turn(n):
                if n >= 2:
                    pe.wait_ge(node_act, n - 1 + 1)
                last = min(2, BLOCKS - 2 * n)
                for j in range(last * 2):
                    ins = T.transpose(tp[:, n % 2, j * P:(j + 1) * P],
                                      nouter[:, 2 * n + j // 2, (j % 2) * 8:(j % 2) * 8 + 8, :]
                                      .rearrange("p i h -> p (i h)"), ident[:])
                ins.then_inc(node_pe, 1)

            def upd_apply(n):
                pe.wait_ge(node_act, n + 2)
                for j in range(min(2, BLOCKS - 2 * n)):
                    blk = 2 * n + j
                    for t in range(2):
                        ins = T.matmul(mm[:, 1, blk * D:(blk + 1) * D],
                                       turned[:, n % 2, (2 * j + t) * P:(2 * j + t + 1) * P],
                                       w_upd[:, t, :], start=(t == 0), stop=(t == 1))
                ins.then_inc(node_pe, 1)

            upd_turn(0)
            for n in range(1, steps):
                upd_turn(n)
                upd_apply(n - 1)
            upd_apply(steps - 1)
            turn_and_apply(aggl, bd_upd, 3, steps + 3)

            pe.wait_ge(sums_out, 3)
            clear_acc(acc2_zero)

            def front2(s, k):
                pe.wait_ge(rows2_in[k], landed(s, k, 2 * CH))

                def turn(q):
                    if not (early(s, 1) and q < 2):
                        pe.wait_ge(xt_out, s * Q + q - 1)
                    for j in range(QC):
                        ins = T.transpose(tp[0:2 * D, q % 2, j * EP:(j + 1) * EP],
                                          gath[:, k, q * QC + j, 1:3, :].rearrange("p a d -> p (a d)"),
                                          ident[0:EP, 0:EP])
                    ins.then_inc(xt_pe, 1)

                def hidden(q):
                    pe.wait_ge(xt_out, s * Q + q + 1)
                    if not (early(s, 1) and q < 2):
                        pe.wait_ge(h_out, s * Q + q - 1)
                    T.matmul(mm[:, q % 2, 0:QC * EP], w1[:], x_t[:, q % 2, 0:QC * EP],
                             start=True, stop=True).then_inc(h_pe, 1)

                def vectors(q):
                    pe.wait_ge(h_out, s * Q + q + 1)
                    if q == 0 and not early(s, 1):
                        pe.wait_ge(v_out, s)
                    for j in range(QC):
                        c = q * QC + j
                        ins = T.matmul(vv[0:EP, c * 2 * D:(c + 1) * 2 * D], h[:, q % 2, j * EP:(j + 1) * EP],
                                       w2[:], start=True, stop=True)
                    ins.then_inc(v_pe, 1)

                turn(0)
                turn(1)
                hidden(0)
                turn(2)
                hidden(1)
                vectors(0)
                turn(3)
                hidden(2)
                vectors(1)
                hidden(3)
                vectors(2)
                vectors(3)

            def back2(s, k):
                for w in range(2):
                    pe.wait_ge(prod2_made, 2 * s + w + 1)
                    for c in range(CH):
                        pe.wait_ge(hot2_made, (2 * s + w) * CH + c + 1)
                        for b in range(NB):
                            ins = T.matmul(acc[:, b // 2, (b % 2) * YG:(b % 2) * YG + YG],
                                           hot[:, c % 4, b * P:(b + 1) * P],
                                           prod2[:, k, w, c].rearrange("p a m -> p (a m)"),
                                           start=False, stop=False, skip_group_check=True)
                        ins.then_inc(hot2_used, 1)

            run_tiles(pe, S, front2, back2)
            T.matmul(vv[0:2, 0:2], zeros[:, 0:2], zeros[:, 0:2], start=True, stop=True).then_inc(acc2_done, 1)

        @block.scalar
        def _(act):
            A = nc.scalar

            def front(s, k):
                for q in range(Q):
                    act.wait_ge(turned_pe, s * Q + q + 1)
                    if not (early(s, 1) and q < 2):
                        act.wait_ge(msg_pe, s * Q + q - 1)
                    A.activation(outer_t[:, q % 2, 0:QC * EP], tp[:, q % 2, 0:QC * EP], ACT.Copy).then_inc(turned_out, 1)
                act.wait_ge(msg_pe, s * Q + Q)
                if not early(s, 2):
                    act.wait_ge(part_made, s - 1)
                A.activation(msg[:, k].rearrange("p c t d -> p (c t d)")[:, 0:CH * D], mm[0:EP, k, 0:CH * D], ACT.Silu,
                             scale=float(KM) ** -0.5).then_inc(msg_made, 1)

            def none(s, k):
                pass

            run_tiles(act, S, front, none)
            act.wait_ge(acc_done, 1)
            for bank in range(3):
                A.activation(sums[:, bank, :], acc[:, bank, :], ACT.Copy).then_inc(sums_out, 1)
            act.wait_ge(node_dve, 1)
            A.activation(root[:], deg[:], ACT.Sqrt).then_inc(root_given, 1)
            act.wait_ge(node_pe, 1)
            A.activation(turned[:, 0, :], tp[:, 0, :], ACT.Copy).then_inc(node_act, 1)
            steps = (BLOCKS + 1) // 2
            for n in range(steps):
                act.wait_ge(node_pe, 3 + (0 if n == 0 else 2 * n - 1))
                if n >= 2:
                    act.wait_ge(node_pe, 3 + 2 * (n - 1))
                w = min(4, 2 * (BLOCKS - 2 * n)) * P
                A.activation(turned[:, n % 2, 0:w], tp[:, n % 2, 0:w], ACT.Copy).then_inc(node_act, 1)
            act.wait_ge(node_pe, 2 + 2 * steps)
            A.activation(aggl[:, 0:BLOCKS, :].rearrange("p b d -> p (b d)"), mm[:, 1, 0:BLOCKS * D], ACT.Silu,
                         scale=float(D * D) ** -0.5).then_inc(node_act, 1)
            act.wait_ge(node_pe, 3 + 2 * steps)
            A.activation(turned[:, 0, :], tp[:, 0, :], ACT.Copy).then_inc(node_act, 1)

            act.wait_ge(root_asked, 1)
            A.activation(root[:], stat[:], ACT.Sqrt).then_inc(root_given, 1)

            def front2(s, k):
                def copy(q):
                    act.wait_ge(xt_pe, s * Q + q + 1)
                    if not (early(s, 1) and q < 2):
                        act.wait_ge(h_pe, s * Q + q - 1)
                    A.activation(x_t[:, q % 2, 0:QC * EP], tp[0:2 * D, q % 2, 0:QC * EP], ACT.Copy).then_inc(xt_out, 1)

                def relu(q):
                    act.wait_ge(h_pe, s * Q + q + 1)
                    if not (early(s, 1) and q < 2):
                        act.wait_ge(v_pe, s * Q + q - 1)
                    A.activation(h[:, q % 2, 0:QC * EP], mm[:, q % 2, 0:QC * EP], ACT.Relu,
                                 bias=bias1[:, 0:1]).then_inc(h_out, 1)

                copy(0)
                copy(1)
                relu(0)
                copy(2)
                relu(1)
                copy(3)
                relu(2)
                relu(3)

            run_tiles(act, S, front2, none)
            act.wait_ge(acc2_done, 1)
            for bank in range(3):
                A.activation(sums[:, bank, :], acc[:, bank, :], ACT.Copy).then_inc(sums2_out, 1)
            act.wait_ge(root_asked, 2)
            A.activation(root[:], stat[:], ACT.Sqrt).then_inc(root_given, 1)

        @block.vector
        def _(dve):
            V = nc.vector
            ch = Chain(dve, setup)
            link = ch.link
            V.memset(zeros[:], 0.0)
            V.memset(xn[:], 0.0)
            V.memset(agg[:], 0.0)
            V.memset(aggl[:], 0.0)
            V.memset(bd_msg[:], 0.0)
            V.memset(bd_upd[:], 0.0)
            V.memset(w2[:], 0.0)
            link(V.memset(parts[:], 1.0))
            dve.wait_ge(iota_made, 2)
            link(V.tensor_copy(part_id[:], iota_p[:]))
            link(V.tensor_scalar(ident[:], iota_n[:, 0:P], part_id[:, 0:1], None, ALU.is_equal))
            V.tensor_scalar(part_id[:], part_id[:], 1.0, None, ALU.mult).then_inc(consts_ready, 1)
            dve.wait_ge(idx_in, 32)
            for t in range(2):
                link(V.tensor_copy(fidx[:], idx[t][:]))
                link(V.tensor_scalar(span[:], fidx[:], float(NT), None, ALU.is_ge))
                for a in range(2, NA):
                    link(V.scalar_tensor_tensor(out=span[:], in0=fidx[:], scalar=float(NT * a), in1=span[:],
                                                op0=ALU.is_ge, op1=ALU.add))
                link(V.scalar_tensor_tensor(out=within[t][:], in0=span[:], scalar=-float(NT), in1=fidx[:],
                                            op0=ALU.mult, op1=ALU.add))
                link(V.tensor_tensor(in_span[t][:], bcast(iota_n[0:EP, 0:NA].unsqueeze(1), (EP, C, NA)),
                                     bcast(span[:].unsqueeze(2), (EP, C, NA)), ALU.is_equal))

            def front(s, k):
                dve.wait_ge(attr_in[k], landed(s, k, 1))
                dve.wait_ge(rows_in[k], landed(s, k, CH))
                if not early(s, 2):
                    dve.wait_ge(turned_pe, (s - 1) * Q)
                V.tensor_tensor(outer[:, k], bcast(xj[:, k].unsqueeze(3), (EP, CH, D, DE)),
                                bcast(attr[:, k].unsqueeze(2), (EP, CH, D, DE)), ALU.mult).then_inc(outer_made, 1)

            schain = Chain(dve, split_chain, 4)

            def back(s, k):
                schain.step(s)
                dve.wait_ge(msg_made, s + 1)
                m = msg[:, k].rearrange("p c t d -> p (c t d)")[:, 0:CH * D].rearrange("p (c d) -> p c d", c=CH)
                r = rest[:].rearrange("p c t d -> p (c t d)")[:, 0:CH * D].rearrange("p (c d) -> p c d", c=CH)
                if not early(s, 1):
                    dve.wait_ge(prod_made, s)
                schain.link(V.tensor_copy(parts[:, :, 0:D], m))
                schain.link(V.tensor_tensor(r, m, parts[:, :, 0:D], ALU.subtract))
                schain.link(V.tensor_copy(parts[:, :, D:2 * D], r))
                schain.link(V.tensor_tensor(r, r, parts[:, :, D:2 * D], ALU.subtract))
                V.tensor_copy(parts[:, :, 2 * D:3 * D], r).then_inc(part_made, 1)
                dve.wait_ge(part_made, s + 1)
                if not early(s, 2):
                    dve.wait_ge(hot_used, (s - 1) * CH)
                V.tensor_tensor(prod[:, k], bcast(in_span[0][:, bass.ds(s * CH, CH), :].unsqueeze(3), (EP, CH, NA, MW)),
                                bcast(parts[:].unsqueeze(2), (EP, CH, NA, MW)), ALU.mult).then_inc(prod_made, 1)
                for c in range(CH):
                    if not (early(s, 1) and c < 4):
                        dve.wait_ge(hot_used, s * CH + c - 3)
                    V.tensor_scalar(dhot[:, c % 4, :], iota_n[0:EP, :], within[1][:, bass.ds(s * CH + c, 1)], None,
                                    ALU.is_equal)
                    V.tensor_scalar(hot[:, c % 4, :], iota_n[0:EP, :], within[0][:, bass.ds(s * CH + c, 1)], None,
                                    ALU.is_equal).then_inc(hot_made, 1)

            run_tiles(dve, S, front, back)

            nch = Chain(dve, node_chain)
            nl = nch.link

            def sum_parts(target, width):
                for b in range(NB):
                    base = sums[:, b // 2, (b % 2) * NA * width:(b % 2 + 1) * NA * width].rearrange(
                        "p (a m) -> p a m", a=NA)
                    t = target[:, b:BLOCKS:NB, :]
                    nl(V.tensor_tensor(t, base[:, :, 0:D], base[:, :, D:2 * D], ALU.add))
                    nl(V.tensor_tensor(t, t, base[:, :, 2 * D:3 * D], ALU.add))

            def inverse_root(value, target, turn):
                dve.wait_ge(root_given, turn)
                nl(V.reciprocal(target, root[:]))
                nl(V.tensor_tensor(newton[:], target, target, ALU.mult))
                nl(V.tensor_tensor(newton[:], newton[:], value, ALU.mult))
                nl(V.tensor_scalar(newton[:], newton[:], -0.5, 1.5, ALU.mult, ALU.add))
                nl(V.tensor_tensor(target, target, newton[:], ALU.mult))

            def layernorm(t, scratch, target, turn):
                b3 = (P, BLOCKS, D)
                nl(V.tensor_reduce(stat[:], t[:], AX, ALU.add))
                nl(V.tensor_scalar(stat[:], stat[:], 1.0 / D, None, ALU.mult))
                nl(V.tensor_tensor(t[:], t[:], bcast(stat[:].unsqueeze(2), b3), ALU.subtract))
                nl(V.tensor_tensor(scratch[:], t[:], t[:], ALU.mult))
                nl(V.tensor_reduce(stat[:], scratch[:], AX, ALU.add))
                V.tensor_scalar(stat[:], stat[:], 1.0 / D, NORM_EPS, ALU.mult, ALU.add).then_inc(root_asked, 1)
                dve.wait_ge(root_asked, turn - 1)
                inverse_root(stat[:], inv[:], turn)
                nl(V.tensor_tensor(target, t[:], bcast(inv[:].unsqueeze(2), b3), ALU.mult))

            dve.wait_ge(sums_out, 3)
            sum_parts(agg, MW)
            for b in range(NB):
                base = sums[:, b // 2, (b % 2) * GW:(b % 2 + 1) * GW].rearrange("p (a m) -> p a m", a=NA)
                nl(V.tensor_tensor(deg[:, b:BLOCKS:NB].unsqueeze(2), base[:, :, MW - 1:MW],
                                   sums[:, 2, GW + b * NA:GW + (b + 1) * NA].unsqueeze(2), ALU.add))
            V.tensor_scalar(deg[:], deg[:], DEG_FLOOR, None, ALU.max).then_inc(node_dve, 1)
            dve.wait_ge(node_dve, 1)
            inverse_root(deg[:], dis[:], 1)
            dve.wait_ge(nodes_in, 32)
            dve.wait_ge(node_pe, 2)
            nl(V.tensor_scalar(aggl[:].rearrange("p b d -> p (b d)"), mm[:, 0, :], float(D) ** -0.5, None, ALU.mult))
            V.tensor_tensor(nouter[:], bcast(xn[:].unsqueeze(3), (P, BLOCKS, D, D)),
                            bcast(aggl[:, 0:BLOCKS, :].unsqueeze(2), (P, BLOCKS, D, D)), ALU.mult).then_inc(node_dve, 1)
            steps = (BLOCKS + 1) // 2
            dve.wait_ge(node_act, 2 + steps)
            V.tensor_copy(stat[:], deg[:]).then_inc(node_dve, 1)
            dve.wait_ge(node_pe, 4 + 2 * steps)
            nl(V.tensor_scalar(tmp[:].rearrange("p b d -> p (b d)"), mm[:, 0, 0:BLOCKS * D], float(D) ** -0.5, None,
                               ALU.mult))
            nl(V.scalar_tensor_tensor(out=tmp[:], in0=xn[:], scalar=2.0, in1=tmp[:], op0=ALU.mult, op1=ALU.add))
            layernorm(tmp, tmp2, x1[:], 2)
            nl(V.tensor_copy(xz[:, :, D:2 * D], x1[:]))
            nl(V.tensor_tensor(xz[:, :, 0:D], x1[:], bcast(dis[:].unsqueeze(2), (P, BLOCKS, D)), ALU.mult))
            V.tensor_copy(xz[:, :, 2 * D:3 * D], xz[:, :, 0:D]).then_inc(table_ready, 1)

            hchain = Chain(dve, house_chain, 13)
            cchain = Chain(dve, split2_chain, 5)
            full = (EP, CH, 2, D)

            def front2(s, k):
                pass

            def edge_math(s, k):
                hchain.step(s)
                lk = hchain.link
                g = gath[:, k]
                z = g[:, :, 0:4:3, :]
                m = msg[:, k]
                dve.wait_ge(v_pe, (s + 1) * Q)
                V.tensor_tensor(v[:], vv[0:EP, :].rearrange("p (c t d) -> p c t d", c=CH, t=2),
                                bcast(bias2[:].unsqueeze(1), full), ALU.add).then_inc(v_out, 1)
                dve.wait_ge(v_out, s + 1)
                dve.wait_ge(rows2_in[k], landed(s, k, 2 * CH))
                lk(V.tensor_tensor(sq[:], v[:], v[:], ALU.mult))
                lk(V.tensor_reduce(rnorm[:], sq[:], AX, ALU.add))
                lk(V.tensor_scalar(rnorm[:], rnorm[:], UNIT_FLOOR ** 2, 0.5, ALU.max, ALU.mult))
                lk(V.reciprocal(rnorm[:], rnorm[:]))
                lk(V.tensor_tensor(sq[:], v[:], z, ALU.mult))
                lk(V.tensor_reduce(scal[:], sq[:], AX, ALU.add))
                lk(V.tensor_tensor(scal[:], scal[:], rnorm[:], ALU.mult))
                lk(V.tensor_tensor(sq[:], v[:], bcast(scal[:].unsqueeze(3), full), ALU.mult))
                lk(V.tensor_tensor(t1[:], z, sq[:], ALU.subtract))
                for w in range(2):
                    ins = V.tensor_tensor(sq[:, :, w, :], v[:, :, w, :], t1[:, :, 1 - w, :], ALU.mult)
                lk(ins)
                lk(V.tensor_reduce(scal[:], sq[:], AX, ALU.add))
                lk(V.tensor_tensor(scal[:], scal[:], rnorm[:], ALU.mult))
                lk(V.tensor_tensor(sq[:], v[:], bcast(scal[:].unsqueeze(3), full), ALU.mult))
                for w in range(2):
                    ins = V.tensor_tensor(m[:, :, w, :], t1[:, :, 1 - w, :], sq[:, :, w, :], ALU.subtract)
                ins.then_inc(msg2_made, 1)
                dve.wait_ge(msg2_made, s + 1)

            def part(i):
                return parts2[:, :, :, i * D:(i + 1) * D].rearrange("p w c d -> p c w d")

            def back2(s, k):
                edge_math(s, k)
                cchain.step(s)
                lk = cchain.link
                m = msg[:, k]
                lk(V.tensor_copy(part(0), m))
                lk(V.tensor_tensor(rest[:], m, part(0), ALU.subtract))
                lk(V.tensor_copy(part(1), rest[:]))
                lk(V.tensor_tensor(rest[:], rest[:], part(1), ALU.subtract))
                lk(V.tensor_copy(part(2), rest[:]))
                if not early(s, 2):
                    dve.wait_ge(hot2_used, (s - 1) * 2 * CH)
                for w in range(2):
                    V.tensor_tensor(prod2[:, k, w],
                                    bcast(in_span[w][:, bass.ds(s * CH, CH), :].unsqueeze(3), (EP, CH, NA, YW)),
                                    bcast(parts2[:, w].unsqueeze(2), (EP, CH, NA, YW)), ALU.mult).then_inc(prod2_made, 1)
                    for c in range(CH):
                        if not (early(s, 1) and w == 0 and c < 4):
                            dve.wait_ge(hot2_used, (2 * s + w) * CH + c - 3)
                        V.tensor_scalar(hot[:, c % 4, :], iota_n[0:EP, :], within[w][:, bass.ds(s * CH + c, 1)], None,
                                        ALU.is_equal).then_inc(hot2_made, 1)

            run_tiles(dve, S, front2, back2)

            dve.wait_ge(sums2_out, 3)
            sum_parts(tmp2, YW)
            nl(V.tensor_tensor(tmp2[:], tmp2[:], bcast(dis[:].unsqueeze(2), (P, BLOCKS, D)), ALU.mult))
            nl(V.tensor_tensor(tmp2[:], tmp2[:], x1[:], ALU.add))
            nl(V.tensor_scalar(tmp2[:], tmp2[:], 0.0, None, ALU.max))
            nl(V.tensor_tensor(tmp[:], tmp2[:], x1[:], ALU.add))
            layernorm(tmp, tmp2, tmp[:], 3)
            V.tensor_copy(stat[:], deg[:]).then_inc(out_ready, 1)


_INS = [("x", "x"), ("src", "src"), ("dst", "dst"), ("edge_attr_8", "edge_attr"),
        ("L0_gnn_W_msg_tp", "w_msg_tp"), ("L0_gnn_W_msg_lin", "w_msg_lin"),
        ("L0_gnn_W_upd_tp", "w_upd_tp"), ("L0_gnn_W_upd_lin", "w_upd_lin"),
        ("L1_gnn_W1", "w1_t"), ("L1_gnn_b1", "b1"), ("L1_gnn_W2", "w2_t"), ("L1_gnn_b2", "b2")]


def kernel(**inputs):
    import numpy as np
    import concourse.bacc as bacc
    from concourse.bass_utils import run_bass_kernel_spmd

    nc = bacc.Bacc("TRN2", target_bir_lowering=False, num_devices=1)
    arrays, args = {}, []
    for given, name in _INS:
        a = np.asarray(inputs[given])
        if name in ("w1_t", "w2_t"):
            a = a.T
        a = np.ascontiguousarray(a)
        arrays[name] = a
        args.append(nc.dram_tensor(name, a.shape, mybir.dt.from_np(a.dtype), kind="ExternalInput").ap())
    shape = inputs["x"].shape
    args.append(nc.dram_tensor("out", shape, F32, kind="ExternalOutput").ap())
    gnn_resnorm_kernel(nc, *args)
    r = run_bass_kernel_spmd(nc, [arrays], core_ids=[0])
    return r.results[0]["out"]
```

```python
from contextlib import ExitStack

import concourse.bass as bass
from concourse import mybir

ALU = mybir.AluOpType
ACT = mybir.ActivationFunctionType
F32 = mybir.dt.float32
BF16 = mybir.dt.bfloat16
I16 = mybir.dt.int16
I32 = mybir.dt.int32
AX = mybir.AxisListType.X

EP = 125
CH = 16
Q = 4
QC = CH // Q
P = 128
NB = 5
NA = 5
BLOCKS = NA * NB
WIN = 2
PADB = 32
LEAD = 6
STEPS = 4
PARTS = 3
NORM_EPS = 1e-5
DEG_FLOOR = 1e-5
UNIT_FLOOR = 1e-12


def bcast(ap, shape):
    return ap.broadcast_to(list(shape))


class Chain:

    def __init__(self, eng, sem, per_step=0):
        self.eng, self.sem, self.per, self.base, self.k = eng, sem, per_step, 0, 0

    def step(self, s):
        assert self.k in (0, self.per)
        self.base, self.k = s * self.per, 0

    def link(self, ins):
        self.k += 1
        ins.then_inc(self.sem, 1)
        self.eng.wait_ge(self.sem, self.base + self.k)


def run_tiles(eng, tiles, front, back):
    for s in range(3):
        front(s, s % 2)
        if s:
            back(s - 1, (s - 1) % 2)
    with eng.Fori(3, tiles - 2, 2) as i:
        front(i, 1)
        back(i - 1, 0)
        front(i + 1, 0)
        back(i, 1)
    front(tiles - 1, 1)
    back(tiles - 2, 0)
    back(tiles - 1, 1)


def run_steps(eng, tiles, step, depth):
    for t in range(LEAD):
        step(t, t)
    with eng.Fori(LEAD, tiles - STEPS + 1, STEPS) as i:
        for u in range(STEPS):
            step(i + u, LEAD + u)
    for t in range(tiles, tiles + depth):
        step(t, t)


def landed(s, k, dmas, slots=2):
    return s * (16 // slots * dmas) + (16 - 16 // slots * k) * dmas


def live(t, j, tiles):
    return -1 if isinstance(t, int) and not 0 <= t - j < tiles else 0


def early(s, n):
    return isinstance(s, int) and s < n


def gnn_resnorm_kernel(nc, x, src, dst, dst_flat, edge_attr, w_msg_tp, w_msg_lin, w_upd_tp, w_upd_lin,
                       w1_t, b1, w2_t, b2, out):
    N, D = x.shape
    E = dst_flat.shape[0]
    DE = edge_attr.shape[2] // CH
    HID = b1.shape[0]
    S = E // (EP * CH)
    C = S * CH
    FULLB, TAIL = N // P, N % P
    KM = D * DE
    MW = PARTS * D + 2
    TE = EP * CH
    RW = D + 1
    HALF = CH // 2
    UPD = (BLOCKS + 1) // 2
    GW = NA * MW
    YW = PARTS * D
    YG = NA * YW
    NT = NB * P
    assert S * EP * CH == E and S % 2 == 0 and (S - LEAD) % STEPS == 0 and KM == P and BLOCKS * P >= N and 2 * HID == P

    with ExitStack() as ctx:
        def sb(name, shape, dt=F32):
            return ctx.enter_context(nc.sbuf_tensor(name, shape, dt))

        def ps(name, shape):
            return ctx.enter_context(nc.psum_tensor(name, shape, F32))

        def sem(name):
            return ctx.enter_context(nc.semaphore(name))

        table_s = nc.dram_tensor("table_s", (BLOCKS * P, 2 * D), F32, kind="Internal").ap()
        dst16 = nc.dram_tensor("dst16", (E,), I16, kind="Internal").ap()
        table_d = nc.dram_tensor("table_d", (BLOCKS * P, 2 * D), F32, kind="Internal").ap()

        acc = ps("acc", [P, 3, 512])
        tp = ps("tp", [P, 2, 512])
        mm = ps("mm", [P, 2, 512])
        vv = ps("vv", [P, 512])

        iota_n = sb("iota_n", [P, NT], I16)
        iota_p = sb("iota_p", [P, 1], I32)
        part_id = sb("part_id", [P, 1])
        ident = sb("ident", [P, P])
        zeros = sb("zeros", [P, 512], BF16)
        w_msg = sb("w_msg", [P, D])
        w_upd = sb("w_upd", [P, 2, D])
        bd_msg = sb("bd_msg", [P, P])
        bd_upd = sb("bd_upd", [P, P])
        w1 = sb("w1", [2 * D, 2 * HID])
        w2 = sb("w2", [2 * HID, 2 * D])
        bias1 = sb("bias1", [2 * HID, 1])
        bias2 = sb("bias2", [EP, 2, D])
        idx = [sb("src_idx", [EP, C], I32), sb("dst_idx", [EP, C], I32)]
        idx_now = sb("idx_now", [EP, 4, 2, CH], I32)
        within = [sb("src_within", [EP, C]), sb("dst_within", [EP, C])]
        near_or_span = sb("near_or_span", [P, 2 * WIN * TE], BF16)
        hot_t = near_or_span[:].rearrange("p (k w e) -> p k w e", k=2, w=WIN)
        in_span = [sb("src_in_span", [EP, C, NA, 2], BF16)[:],
                   near_or_span[0:EP, 0:C * NA * 2].rearrange("p (c a t) -> p c a t", a=NA, t=2)]
        xn = sb("xn", [P, BLOCKS, D])
        agg = sb("agg", [P, PADB, D])
        aggl = sb("aggl", [P, PADB, D])
        deg = sb("deg", [P, BLOCKS])
        dis = sb("dis", [P, BLOCKS])
        tmp = sb("tmp", [P, BLOCKS, D])
        tmp2 = sb("tmp2", [P, BLOCKS, D])
        stat = sb("stat", [P, BLOCKS])
        root = sb("root", [P, BLOCKS])
        inv = sb("inv", [P, BLOCKS])
        newton = sb("newton", [P, BLOCKS])
        x1 = sb("x1", [P, BLOCKS, D])
        xz = sb("xz", [P, BLOCKS, 3 * D])
        hot_space = sb("hot_space", [P, 2 * CH * NT], BF16)
        hots = hot_space[0:EP, :].rearrange("p (k c n) -> p k c n", k=2, c=CH)
        space32 = hot_space[:].bitcast(F32)
        nouter = space32[:, 0:BLOCKS * D * D].rearrange("p (b i h) -> p b i h", b=BLOCKS, i=D)
        turned = space32[:, BLOCKS * D * D:BLOCKS * D * D + 1024].rearrange("p (t n) -> p t n", t=2)
        sums = space32[:, BLOCKS * D * D + 1024:BLOCKS * D * D + 1024 + 1536].rearrange("p (t n) -> p t n", t=3)
        fidx = space32[0:EP, 0:C]
        span = space32[0:EP, C:2 * C]
        dst_int = space32[0:EP, 2 * C:3 * C].bitcast(I32)
        dst_short = sb("dst_short", [EP, C], I16)
        ends = sb("ends", [EP, 2, S])
        end_col = sb("end_col", [2 * S, 1])
        end_row = sb("end_row", [1, 2, S])
        block_start = sb("block_start", [1, BLOCKS - 1], I16)
        passed = space32[0:1, 3 * C:3 * C + S * (BLOCKS - 1)].rearrange("p (s b) -> p s b", s=S)
        base = sb("base", [1, S])
        near_row = sb("near_row", [1, S])
        base_i = sb("base_i", [1, S], I32)
        near = sb("near", [1, 1])
        near_i = sb("near_i", [1, 1], I32)
        base_row = sb("base_row", [1, S, WIN])
        ones_row = sb("ones_row", [1, P])
        base_col = sb("base_col", [S * WIN, 1])
        window = sb("window", [P, S, WIN])
        counts = sb("counts", [P, S, WIN])
        counts_t = sb("counts_t", [S * WIN, P])
        select = sb("select", [S * WIN, BLOCKS])
        dst_all = sb("dst_all", [P, 2, TE], I16)
        rows_tab = sb("rows_tab", [P, BLOCKS + WIN - 1, PARTS, RW], BF16)
        win_tab = sb("win_tab", [P, 2, WIN, PARTS * RW], BF16)
        wsum = sb("wsum", [P, BLOCKS + WIN - 1, PARTS * D])
        count_junk = wsum[:].rearrange("p b m -> p (b m)")[:, 0:TE // 2].bitcast(BF16)
        wtile = sb("wtile", [P, WIN * PARTS * D])
        picked = sb("picked", [EP, CH, PARTS, RW])
        dis_e = sb("dis_e", [EP, CH])
        attr = sb("attr", [EP, 2, CH, DE])
        xj = sb("xj", [EP, 2, CH, D])
        edge_space = sb("edge_space", [EP, 2 * CH * D * DE])
        outer = edge_space[:].rearrange("p (k c i j) -> p k c i j", k=2, c=CH, i=D)
        gath = edge_space[:].rearrange("p (k c f d) -> p k c f d", k=4, c=CH, f=4)
        outer_t = sb("outer_t", [P, 2, 512])
        msg = sb("msg", [EP, 2, CH, 2, D])
        rest = sb("rest", [EP, CH, 2, D])
        parts = sb("parts", [EP, CH, MW], BF16)
        parts2 = sb("parts2", [EP, 2, 2, CH, YW], BF16)
        prod_space = sb("prod_space", [EP, 2 * CH * NA * MW], BF16)
        prod = prod_space[:].rearrange("p (k c a m) -> p k c a m", k=2, c=CH, a=NA)
        prod2 = prod_space[:, 0:2 * CH * NA * YW].rearrange("p (k c a m) -> p k c a m", k=2, c=CH, a=NA)
        win_hots = sb("win_hots", [EP, 2 * CH * WIN * P], BF16)
        win_hot = win_hots[:].rearrange("p (k c n) -> p k c n", k=2, c=CH)
        hot = hots[:, 0]
        dhot = win_hots[:, 0:4 * NT].rearrange("p (c n) -> p c n", c=4)
        x_t = sb("x_t", [2 * D, 2, 512])
        h = outer_t
        v = xj[:].rearrange("p k c d -> p (k c d)").rearrange("p (c t d) -> p c t d", c=CH, t=2)
        sq = sb("sq", [EP, CH, 2, D])
        t1 = sb("t1", [EP, CH, 2, D])
        scal = sb("scal", [EP, CH, 2])
        rnorm = sb("rnorm", [EP, CH, 2])

        idx_in = sem("idx_in")
        nodes_in = sem("nodes_in")
        weights_in = sem("weights_in")
        iota_made = sem("iota_made")
        dst16_made = sem("dst16_made")
        dst16_out = sem("dst16_out")
        ends_dve = sem("ends_dve")
        ends_pe = sem("ends_pe")
        near_known = sem("near_known")
        dst_in = [sem("dst_in0"), sem("dst_in1")]
        dst2_in = [sem("dst2_in0"), sem("dst2_in1")]
        near_rows = [sem(f"near_rows{i}") for i in range(4)]
        tab_made = sem("tab_made")
        hot_t_made = sem("hot_t_made")
        win_tab_made = sem("win_tab_made")
        picked_pe = sem("picked_pe")
        picked_out = sem("picked_out")
        counted = sem("counted")
        xj_made = sem("xj_made")
        xj_chain = sem("xj_chain")
        scattered = sem("scattered")
        hots_made = sem("hots_made")
        cnt_pe = sem("cnt_pe")
        cnt_out = sem("cnt_out")
        hot_t2_made = sem("hot_t2_made")
        win_tab2_made = sem("win_tab2_made")
        picked2_pe = sem("picked2_pe")
        picked2_out = sem("picked2_out")
        rows_made = sem("rows_made")
        rows_chain = sem("rows_chain")
        scattered2 = sem("scattered2")
        hots2_made = sem("hots2_made")
        wtile_out = sem("wtile_out")
        wsum_added = sem("wsum_added")
        setup = sem("setup")
        indices_ready = sem("indices_ready")
        consts_ready = sem("consts_ready")
        root_asked = sem("root_asked")
        root_given = sem("root_given")
        pool_held = sem("pool_held")
        idx_placed = sem("idx_placed")
        idx2_placed = sem("idx2_placed")
        attr_in = [sem("attr_in0"), sem("attr_in1")]
        rows_in = [sem("rows_in0"), sem("rows_in1")]
        outer_made = sem("outer_made")
        turned_pe = sem("turned_pe")
        turned_out = sem("turned_out")
        msg_pe = sem("msg_pe")
        msg_made = sem("msg_made")
        part_made = sem("part_made")
        split_chain = sem("split_chain")
        prod_made = sem("prod_made")
        hot_made = sem("hot_made")
        dhot_made = sem("dhot_made")
        hot_used = sem("hot_used")
        prod_used = sem("prod_used")
        acc_zero = sem("acc_zero")
        acc_done = sem("acc_done")
        sums_out = sem("sums_out")
        node_pe = sem("node_pe")
        node_act = sem("node_act")
        node_dve = sem("node_dve")
        node_chain = sem("node_chain")
        table_ready = sem("table_ready")
        table_out = sem("table_out")
        rows2_in = [sem("rows2_in0"), sem("rows2_in1")]
        xt_pe = sem("xt_pe")
        xt_out = sem("xt_out")
        h_pe = sem("h_pe")
        h_out = sem("h_out")
        v_pe = sem("v_pe")
        v_out = sem("v_out")
        msg2_made = sem("msg2_made")
        house_chain = sem("house_chain")
        split2_chain = sem("split2_chain")
        prod2_made = sem("prod2_made")
        hot2_made = sem("hot2_made")
        hot2_used = sem("hot2_used")
        prod2_used = sem("prod2_used")
        acc2_zero = sem("acc2_zero")
        acc2_done = sem("acc2_done")
        sums2_out = sem("sums2_out")
        out_ready = sem("out_ready")
        out_stored = sem("out_stored")

        x_lo = x[0:FULLB * P, :].rearrange("(h p) d -> p h d", p=P)
        out_lo = out[0:FULLB * P, :].rearrange("(h p) d -> p h d", p=P)
        N_WEIGHT_DMAS = 2 + 16 + 3 + 2 + 2 + 2

        block = ctx.enter_context(nc.Block())

        @block.sync
        def _(sp):
            sp.dma_start(idx[0][:], src).then_inc(idx_in, 16)
            sp.dma_start(idx[1][:], dst).then_inc(idx_in, 16)
            sp.dma_start(dst_int, dst_flat.rearrange("(p k) -> p k", p=EP)).then_inc(idx_in, 16)

            def load_attr(s, k):
                sp.dma_start(attr[:, k].rearrange("p c j -> p (c j)"),
                             edge_attr[bass.ds(s, 1)].rearrange("o p f -> (o p) f")).then_inc(attr_in[k], 16)

            load_attr(0, 0)
            load_attr(1, 1)
            sp.wait_ge(consts_ready, 1)
            sp.dma_start(xn[:, 0:FULLB, :], x_lo).then_inc(nodes_in, 16)
            sp.dma_start(xn[0:TAIL, FULLB, :], x[FULLB * P:N, :]).then_inc(nodes_in, 16)
            sp.dma_start(w_msg[:], w_msg_tp.rearrange("i j h -> (i j) h")).then_inc(weights_in, 16)
            sp.dma_start(w_upd[:], w_upd_tp.rearrange("(t i) h k -> (i h) t k", t=2)).then_inc(weights_in, 16)
            for g in range(8):
                r = slice(g * D, (g + 1) * D)
                sp.dma_start(bd_msg[r, r], w_msg_lin).then_inc(weights_in, 16)
                sp.dma_start(bd_upd[r, r], w_upd_lin).then_inc(weights_in, 16)
            sp.dma_start(w1[:, 0:HID], w1_t).then_inc(weights_in, 16)
            sp.dma_start(w1[0:D, HID:2 * HID], w1_t[D:2 * D, :]).then_inc(weights_in, 16)
            sp.dma_start(w1[D:2 * D, HID:2 * HID], w1_t[0:D, :]).then_inc(weights_in, 16)
            for g in range(2):
                sp.dma_start(w2[g * HID:(g + 1) * HID, g * D:(g + 1) * D], w2_t).then_inc(weights_in, 16)
                sp.dma_start(bias1[g * HID:(g + 1) * HID, :], b1.unsqueeze(1)).then_inc(weights_in, 16)
                sp.dma_start(bias2[:, g, :], bcast(b2.unsqueeze(0), (EP, D))).then_inc(weights_in, 16)
            sp.wait_ge(dst16_made, 1)
            sp.dma_start(dst16.rearrange("(p k) -> p k", p=EP), dst_short[:]).then_inc(dst16_out, 16)
            sp.wait_ge(dst16_out, 16)

            def load_dst(s, k, landed_in):
                sp.dma_start(dst_all[:, k, :],
                             bcast(dst16.rearrange("(s e) -> s e", s=S)[bass.ds(s, 1), :], (P, TE))).then_inc(landed_in[k], 16)

            sp.wait_ge(near_known, 1)
            is_near = sp.value_load(near_i[0:1, 0:1], min_val=0, max_val=1)
            with sp.If(is_near == 1):
                load_dst(0, 0, dst_in)
                load_dst(1, 1, dst_in)
                with sp.Fori(2, S - 1, 2) as i:
                    for k in range(2):
                        sp.wait_ge(hot_t_made, WIN * (i + k - 1))
                        load_dst(i + k, k, dst_in)
                        sp.wait_ge(outer_made, i + k - 1)
                        load_attr(i + k, k)
                sp.wait_ge(hot_t_made, WIN * S)
                load_dst(0, 0, dst2_in)
                load_dst(1, 1, dst2_in)
                sp.wait_ge(table_ready, 1)
                sp.dma_start(table_s.rearrange("(h p) f -> p h f", p=P), xz[:, :, 0:2 * D]).then_inc(table_out, 16)
                with sp.Fori(2, S - 1, 2) as i:
                    for k in range(2):
                        sp.wait_ge(hot_t2_made, WIN * (i + k - 1))
                        load_dst(i + k, k, dst2_in)
            with sp.Else():
                with sp.Fori(2, S - 1, 2) as i:
                    for k in range(2):
                        sp.wait_ge(outer_made, i + k - 1)
                        load_attr(i + k, k)
                sp.wait_ge(table_ready, 1)
                sp.dma_start(table_s.rearrange("(h p) f -> p h f", p=P), xz[:, :, 0:2 * D]).then_inc(table_out, 16)
                sp.dma_start(table_d.rearrange("(h p) f -> p h f", p=P), xz[:, :, D:3 * D]).then_inc(table_out, 16)
            sp.wait_ge(out_ready, 1)
            sp.dma_start(out_lo, tmp[:, 0:FULLB, :]).then_inc(out_stored, 16)
            sp.dma_start(out[FULLB * P:N, :], tmp[0:TAIL, FULLB, :]).then_inc(out_stored, 16)
            sp.wait_ge(out_stored, 32)

        @block.gpsimd
        def _(pool):
            nc.gpsimd.iota(iota_n[:], [[1, NT]], base=0, channel_multiplier=0).then_inc(iota_made, 1)
            nc.gpsimd.iota(iota_p[:], [[0, 1]], base=0, channel_multiplier=1).then_inc(iota_made, 1)
            nc.gpsimd.iota(block_start[:], [[P, BLOCKS - 1]], base=P, channel_multiplier=0).then_inc(iota_made, 1)
            pool.wait_ge(idx_in, 48)

            def hold(signal, count):
                pool.wait_ge(signal, count)
                pool.sem_inc(pool_held, 1)

            def gather(rows, table, which, k, c, signal):
                nc.gpsimd.indirect_dma_start(
                    rows, None, table, bass.IndirectOffsetOnAxis(ap=idx_now[:, k, which, c:c + 1], axis=0)
                ).then_inc(signal, 16)

            def place_indices(which, s, k, copied, count):
                nc.gpsimd.tensor_copy(idx_now[:, k, which, :],
                                      idx[which][:, bass.ds(s * CH, CH)]).then_inc(copied, 1)
                hold(copied, count)

            def first_rows(s, k):
                if not early(s, 2):
                    hold(outer_made, s - 1)
                place_indices(1, s, k, idx_placed, s + 1)
                for c in range(CH):
                    gather(xj[:, k, c, :], x, 1, k, c, rows_in[k])


            def second_rows(s, k):
                if not early(s, 2):
                    hold(msg2_made, s - 1)
                place_indices(0, s, k, idx2_placed, s * 2 + 1)
                place_indices(1, s, k, idx2_placed, s * 2 + 2)
                for c in range(CH):
                    gather(gath[:, k, c, 0:2, :].rearrange("p a d -> p (a d)"), table_s, 0, k, c, rows2_in[k])
                    gather(gath[:, k, c, 2:4, :].rearrange("p a d -> p (a d)"), table_d, 1, k, c, rows2_in[k])

            def source_rows(s, r):
                if not early(s, 4):
                    hold(msg2_made, s - 3)
                place_indices(0, s, r, idx2_placed, s + 1)
                for c in range(CH):
                    gather(gath[:, r, c, 0:2, :].rearrange("p a d -> p (a d)"), table_s, 0, r, c, near_rows[r])

            pool.wait_ge(near_known, 1)
            is_near = pool.value_load(near_i[0:1, 0:1], min_val=0, max_val=1)
            with pool.If(is_near == 1):
                pool.wait_ge(table_out, 16)
                for s in range(LEAD):
                    source_rows(s, s % 4)
                with pool.Fori(LEAD, S - STEPS + 1, STEPS) as i:
                    for u in range(STEPS):
                        source_rows(i + u, (LEAD + u) % 4)
            with pool.Else():
                first_rows(0, 0)
                first_rows(1, 1)
                with pool.Fori(2, S - 1, 2) as i:
                    first_rows(i, 0)
                    first_rows(i + 1, 1)
                pool.wait_ge(table_out, 32)
                second_rows(0, 0)
                second_rows(1, 1)
                with pool.Fori(2, S - 1, 2) as i:
                    second_rows(i, 0)
                    second_rows(i + 1, 1)

        @block.tensor
        def _(pe):
            T = nc.tensor

            def clear_acc(done):
                for bank in range(3):
                    ins = T.matmul(acc[:, bank, :], zeros[:, 0:P], zeros[:], start=True, stop=False,
                                   skip_group_check=True)
                ins.then_inc(done, 1)

            def find_windows():
                pe.wait_ge(ends_dve, 1)
                T.transpose(tp[0:2 * S, 0, 0:EP], ends[:].rearrange("p t s -> p (t s)"),
                            ident[0:EP, 0:EP]).then_inc(ends_pe, 1)
                pe.wait_ge(ends_dve, 2)
                T.transpose(tp[0:1, 1, 0:2 * S], end_col[:], ident[0:2 * S, 0:2 * S]).then_inc(ends_pe, 1)
                pe.wait_ge(ends_dve, 3)
                row = base_row[:].rearrange("p s w -> p (s w)")
                T.matmul(mm[:, 0, 0:S * WIN], ones_row[:], row, start=True, stop=True)
                T.transpose(mm[0:S * WIN, 1, 0:1], row, ident[0:1, 0:1]).then_inc(ends_pe, 1)

            def turn(s, k, q):
                if q == 0:
                    pe.wait_ge(outer_made, s + 1)
                if not (early(s, 1) and q < 2):
                    pe.wait_ge(turned_out, s * Q + q - 1)
                for j in range(QC):
                    ins = T.transpose(tp[:, q % 2, j * EP:(j + 1) * EP],
                                      outer[:, k, q * QC + j].rearrange("p i j -> p (i j)"), ident[0:EP, 0:EP])
                ins.then_inc(turned_pe, 1)

            def messages(s, k, q, slot):
                pe.wait_ge(turned_out, s * Q + q + 1)
                if q == 0 and not early(s, 1 + slot):
                    pe.wait_ge(msg_made, s - slot)
                for j in range(QC):
                    c = q * QC + j
                    ins = T.matmul(mm[0:EP, k * slot, c * D:(c + 1) * D], outer_t[:, q % 2, j * EP:(j + 1) * EP],
                                   w_msg[:], start=True, stop=True)
                ins.then_inc(msg_pe, 1)

            def pick(s, k, half, bank, width, onehots, tables, out_sem, done):
                if half == 0:
                    pe.wait_ge(onehots, WIN * (s + 1))
                    pe.wait_ge(tables, s + 1)
                if bank[1] == 2:
                    if not early(s, 1):
                        pe.wait_ge(out_sem, 2 * s + half - 1)
                elif not (early(s, 1) and half == 0):
                    pe.wait_ge(out_sem, 2 * s + half)
                for c in range(half * HALF, (half + 1) * HALF):
                    for w in range(WIN):
                        ins = T.matmul(bank[0][0:EP, (c % HALF) * width:(c % HALF + 1) * width],
                                       hot_t[:, k, w, c * EP:(c + 1) * EP],
                                       win_tab[:, k, w, 0:width], start=(w == 0), stop=(w == WIN - 1))
                ins.then_inc(done, 1)

            def add_sources(s, k, chunks, products, made, onehots, done):
                if chunks.start == 0:
                    pe.wait_ge(made, s + 1)
                    pe.wait_ge(onehots, s + 1)
                width = NA * products.shape[-1]
                for c in chunks:
                    for b in range(NB):
                        ins = T.matmul(acc[:, b // 2, (b % 2) * width:(b % 2) * width + width],
                                       hots[:, k, c, b * P:(b + 1) * P],
                                       products[:, k, c].rearrange("p a m -> p (a m)"),
                                       start=False, stop=False, skip_group_check=True)
                if chunks.stop == CH and done is not None:
                    ins.then_inc(done, 1)

            def near_first(t, r):
                def turn_if(q):
                    if 0 <= live(t, 1, S):
                        turn(t - 1, (r - 1) % 2, q)

                def msg_if(q):
                    if 0 <= live(t, 1, S):
                        messages(t - 1, (r - 1) % 2, q, 0)

                def pick_if(half):
                    if 0 <= live(t, 0, S):
                        pick(t, r % 2, half, ((mm[:, 1, :], vv)[half], 2), PARTS * D, hot_t_made, win_tab_made,
                             picked_out, picked_pe)

                def add_if(first, last):
                    if 0 <= live(t, 3, S):
                        add_sources(t - 3, (r - 3) % 2, range(first, last), prod, prod_made, hots_made, scattered)

                add_if(0, 2)
                turn_if(0)
                add_if(2, 4)
                turn_if(1)
                add_if(4, 5)
                msg_if(0)
                add_if(5, 7)
                turn_if(2)
                add_if(7, 8)
                msg_if(1)
                add_if(8, 10)
                turn_if(3)
                add_if(10, 11)
                msg_if(2)
                add_if(11, 12)
                pick_if(0)
                add_if(12, 14)
                msg_if(3)
                pick_if(1)
                add_if(14, 16)

            def near_second(t, r):
                s = t - 1
                k = (r - 1) % 2

                def turn2(q):
                    if live(t, 1, S) < 0:
                        return
                    if q == 0:
                        pe.wait_ge(near_rows[(r - 1) % 4], landed(s, (r - 1) % 4, CH, 4))
                        pe.wait_ge(rows_made, s + 1)
                    if not (early(s, 1) and q == 0):
                        pe.wait_ge(xt_out, s * Q + q)
                    for j in range(QC):
                        ins = T.transpose(tp[0:2 * D, 0, j * EP:(j + 1) * EP],
                                          gath[:, (r - 1) % 4, q * QC + j, 1:3, :].rearrange("p a d -> p (a d)"),
                                          ident[0:EP, 0:EP])
                    ins.then_inc(xt_pe, 1)

                def hidden(q):
                    if live(t, 1, S) < 0:
                        return
                    pe.wait_ge(xt_out, s * Q + q + 1)
                    if not (early(s, 1) and q == 0):
                        pe.wait_ge(h_out, s * Q + q)
                    T.matmul(mm[:, 0, 0:QC * EP], w1[:], x_t[:, q % 2, 0:QC * EP],
                             start=True, stop=True).then_inc(h_pe, 1)

                def vectors(q):
                    if live(t, 1, S) < 0:
                        return
                    pe.wait_ge(h_out, s * Q + q + 1)
                    if q == 0 and not early(s, 1):
                        pe.wait_ge(v_out, s)
                    for j in range(QC):
                        c = q * QC + j
                        ins = T.matmul(vv[0:EP, c * 2 * D:(c + 1) * 2 * D], h[:, q % 2, j * EP:(j + 1) * EP],
                                       w2[:], start=True, stop=True)
                    ins.then_inc(v_pe, 1)

                def pick2(half):
                    if 0 <= live(t, 0, S):
                        pick(t, r % 2, half, (tp[:, 1, :], 1), PARTS * RW, hot_t2_made, win_tab2_made,
                             picked2_out, picked2_pe)

                def add(first, last):
                    if live(t, 3, S) < 0:
                        return
                    s3, k3 = t - 3, (r - 3) % 2
                    add_sources(s3, k3, range(first, last), prod2, prod2_made, hots2_made, None)
                    if first == 0 and not early(s3, 1):
                        pe.wait_ge(wtile_out, s3)
                    for c in range(first, last):
                        for w in range(WIN):
                            ins = T.matmul(mm[:, 1, w * YW:(w + 1) * YW], win_hot[:, k3, c, w * P:(w + 1) * P],
                                           parts2[:, k3, 1, c, :], start=(c == 0 and w == 0),
                                           stop=False, skip_group_check=True)
                    if last == CH:
                        ins.then_inc(scattered2, 1)

                add(0, 3)
                turn2(0)
                add(3, 5)
                hidden(0)
                turn2(1)
                add(5, 7)
                vectors(0)
                hidden(1)
                turn2(2)
                add(7, 9)
                vectors(1)
                hidden(2)
                turn2(3)
                add(9, 11)
                vectors(2)
                hidden(3)
                pick2(0)
                add(11, 13)
                vectors(3)
                add(13, 14)
                pick2(1)
                add(14, 16)

            def front(s, k):
                for q in range(Q):
                    turn(s, k, q)
                    if q >= 1:
                        messages(s, k, q - 1, 1)
                messages(s, k, Q - 1, 1)

            def back(s, k):
                pe.wait_ge(prod_made, s + 1)
                for c in range(CH):
                    pe.wait_ge(hot_made, s * CH + c + 1)
                    for b in range(NB):
                        ins = T.matmul(acc[:, b // 2, (b % 2) * GW:(b % 2) * GW + GW],
                                       hot[:, c % 4, b * P:(b + 1) * P],
                                       prod[:, k, c].rearrange("p a m -> p (a m)"),
                                       start=False, stop=False, skip_group_check=True)
                    for b in range(NB):
                        ins = T.matmul(acc[:, 2, GW + b * NA:GW + (b + 1) * NA],
                                       dhot[:, c % 4, b * P:(b + 1) * P],
                                       in_span[1][:, bass.ds(s * CH + c, 1), :, 0].rearrange("p o a -> p (o a)"),
                                       start=False, stop=False, skip_group_check=True)
                    ins.then_inc(hot_used, 1)

            def front2(s, k):
                pe.wait_ge(rows2_in[k], landed(s, k, 2 * CH))

                def turn2(q):
                    if not (early(s, 1) and q < 2):
                        pe.wait_ge(xt_out, s * Q + q - 1)
                    for j in range(QC):
                        ins = T.transpose(tp[0:2 * D, q % 2, j * EP:(j + 1) * EP],
                                          gath[:, k, q * QC + j, 1:3, :].rearrange("p a d -> p (a d)"),
                                          ident[0:EP, 0:EP])
                    ins.then_inc(xt_pe, 1)

                def hidden(q):
                    pe.wait_ge(xt_out, s * Q + q + 1)
                    if not (early(s, 1) and q < 2):
                        pe.wait_ge(h_out, s * Q + q - 1)
                    T.matmul(mm[:, q % 2, 0:QC * EP], w1[:], x_t[:, q % 2, 0:QC * EP],
                             start=True, stop=True).then_inc(h_pe, 1)

                def vectors(q):
                    pe.wait_ge(h_out, s * Q + q + 1)
                    if q == 0 and not early(s, 1):
                        pe.wait_ge(v_out, s)
                    for j in range(QC):
                        c = q * QC + j
                        ins = T.matmul(vv[0:EP, c * 2 * D:(c + 1) * 2 * D], h[:, q % 2, j * EP:(j + 1) * EP],
                                       w2[:], start=True, stop=True)
                    ins.then_inc(v_pe, 1)

                turn2(0)
                turn2(1)
                hidden(0)
                turn2(2)
                hidden(1)
                vectors(0)
                turn2(3)
                hidden(2)
                vectors(1)
                hidden(3)
                vectors(2)
                vectors(3)

            def back2(s, k):
                for w in range(2):
                    pe.wait_ge(prod2_made, 2 * s + w + 1)
                    for c in range(CH):
                        pe.wait_ge(hot2_made, (2 * s + w) * CH + c + 1)
                        for b in range(NB):
                            ins = T.matmul(acc[:, b // 2, (b % 2) * YG:(b % 2) * YG + YG],
                                           hot[:, c % 4, b * P:(b + 1) * P],
                                           prod2[:, w, c].rearrange("p a m -> p (a m)"),
                                           start=False, stop=False, skip_group_check=True)
                        ins.then_inc(hot2_used, 1)

            def turn_and_apply(source, weights, ready, first):
                pe.wait_ge(node_dve, ready)
                for g in range(4):
                    ins = T.transpose(tp[:, 0, g * P:(g + 1) * P],
                                      source[:, g * 8:(g + 1) * 8, :].rearrange("p g d -> p (g d)"), ident[:])
                ins.then_inc(node_pe, 1)
                pe.wait_ge(node_act, first)
                for g in range(4):
                    ins = T.matmul(mm[:, 0, g * P:(g + 1) * P], turned[:, 0, g * P:(g + 1) * P], weights[:],
                                   start=True, stop=True)
                ins.then_inc(node_pe, 1)

            def upd_turn(n):
                if n >= 2:
                    pe.wait_ge(node_act, n)
                last = min(2, BLOCKS - 2 * n)
                for j in range(last * 2):
                    ins = T.transpose(tp[:, n % 2, j * P:(j + 1) * P],
                                      nouter[:, 2 * n + j // 2, (j % 2) * 8:(j % 2) * 8 + 8, :]
                                      .rearrange("p i h -> p (i h)"), ident[:])
                ins.then_inc(node_pe, 1)

            def upd_apply(n):
                pe.wait_ge(node_act, n + 2)
                for j in range(min(2, BLOCKS - 2 * n)):
                    blk = 2 * n + j
                    for half in range(2):
                        ins = T.matmul(mm[:, 1, blk * D:(blk + 1) * D],
                                       turned[:, n % 2, (2 * j + half) * P:(2 * j + half + 1) * P],
                                       w_upd[:, half, :], start=(half == 0), stop=(half == 1))
                ins.then_inc(node_pe, 1)

            def node_update():
                turn_and_apply(agg, bd_msg, 1, 1)
                pe.wait_ge(node_dve, 2)
                upd_turn(0)
                for n in range(1, UPD):
                    upd_turn(n)
                    upd_apply(n - 1)
                upd_apply(UPD - 1)
                turn_and_apply(aggl, bd_upd, 3, UPD + 3)
                pe.wait_ge(sums_out, 3)
                clear_acc(acc2_zero)

            def mark(done):
                T.matmul(vv[0:2, 0:2], zeros[:, 0:2], zeros[:, 0:2], start=True, stop=True).then_inc(done, 1)

            pe.wait_ge(consts_ready, 1)
            clear_acc(acc_zero)
            find_windows()
            pe.wait_ge(weights_in, 16 * N_WEIGHT_DMAS)
            pe.wait_ge(near_known, 1)
            is_near = pe.value_load(near_i[0:1, 0:1], min_val=0, max_val=1)
            with pe.If(is_near == 1):
                run_steps(pe, S, near_first, 3)
                mark(acc_done)
                pe.wait_ge(cnt_out, 1)
                T.transpose(tp[0:S * WIN, 1, 0:P], counts[:].rearrange("p s w -> p (s w)"), ident[:]).then_inc(cnt_pe, 1)
                pe.wait_ge(cnt_out, 2)
                T.matmul(tp[:, 1, 0:BLOCKS], counts_t[:], select[:], start=True, stop=True).then_inc(cnt_pe, 1)
                node_update()
                run_steps(pe, S, near_second, 3)
                mark(acc2_done)
            with pe.Else():
                run_tiles(pe, S, front, back)
                mark(acc_done)
                node_update()
                run_tiles(pe, S, front2, back2)
                mark(acc2_done)

        @block.scalar
        def _(act):
            A = nc.scalar

            def out_messages(s, k, slot):
                for q in range(Q):
                    act.wait_ge(turned_pe, s * Q + q + 1)
                    if not (early(s, 1) and q < 2):
                        act.wait_ge(msg_pe, s * Q + q - 1)
                    A.activation(outer_t[:, q % 2, 0:QC * EP], tp[:, q % 2, 0:QC * EP], ACT.Copy).then_inc(turned_out, 1)
                act.wait_ge(msg_pe, s * Q + Q)
                if not early(s, 2):
                    act.wait_ge(part_made, s - 1)
                A.activation(msg[:, k].rearrange("p c t d -> p (c t d)")[:, 0:CH * D],
                             mm[0:EP, k * slot, 0:CH * D], ACT.Silu,
                             scale=float(KM) ** -0.5).then_inc(msg_made, 1)

            def place_window(s, k, width, picked, made):
                if not early(s, 2):
                    act.wait_ge(picked, 2 * (s - 1))
                first = act.value_load(base_i[0:1, bass.ds(s, 1)], min_val=0, max_val=BLOCKS - 1)
                A.activation(win_tab[:, k, :, 0:width],
                             rows_tab[:].rearrange("p b t r -> p b (t r)")[:, bass.ds(first, WIN), 0:width],
                             ACT.Copy).then_inc(made, 1)

            def copy_picked(s, banks, width, pe_sem, out_sem):
                for half in range(2):
                    act.wait_ge(pe_sem, 2 * s + half + 1)
                    if half == 0 and not early(s, 1):
                        act.wait_ge(rows_made if width == PARTS * RW else xj_made, s)
                    A.activation(picked[:].rearrange("p c t r -> p (c t r)")[:, half * HALF * width:(half + 1) * HALF * width],
                                 banks[half][0:EP, 0:HALF * width], ACT.Copy).then_inc(out_sem, 1)

            def near_first(t, r):
                if 0 <= live(t, 0, S):
                    place_window(t, r % 2, PARTS * D, picked_pe, win_tab_made)
                if 0 <= live(t, 1, S):
                    out_messages(t - 1, (r - 1) % 2, 0)
                if 0 <= live(t, 0, S):
                    copy_picked(t, (mm[:, 1, :], vv), PARTS * D, picked_pe, picked_out)
                    act.wait_ge(hot_t_made, WIN * (t + 1))
                    for w in range(WIN):
                        if not (early(t, 1) and w == 0):
                            act.wait_ge(counted, WIN * t + w)
                        A.activation(count_junk, hot_t[:, r % 2, w, :], ACT.Copy,
                                     accum_out=counts[:, bass.ds(t, 1), w]).then_inc(counted, 1)

            def near_second(t, r):
                s = t - 1

                def copy(q):
                    act.wait_ge(xt_pe, s * Q + q + 1)
                    if not (early(s, 1) and q < 2):
                        act.wait_ge(h_pe, s * Q + q - 1)
                    A.activation(x_t[:, q % 2, 0:QC * EP], tp[0:2 * D, 0, 0:QC * EP], ACT.Copy).then_inc(xt_out, 1)

                def relu(q):
                    act.wait_ge(h_pe, s * Q + q + 1)
                    if not (early(s, 1) and q < 2):
                        act.wait_ge(v_pe, s * Q + q - 1)
                    A.activation(h[:, q % 2, 0:QC * EP], mm[:, 0, 0:QC * EP], ACT.Relu,
                                 bias=bias1[:, 0:1]).then_inc(h_out, 1)

                if 0 <= live(t, 0, S):
                    place_window(t, r % 2, PARTS * RW, picked2_pe, win_tab2_made)
                if 0 <= live(t, 1, S):
                    for q in range(Q):
                        copy(q)
                        relu(q)
                if 0 <= live(t, 0, S):
                    copy_picked(t, (tp[:, 1, :], tp[:, 1, :]), PARTS * RW, picked2_pe, picked2_out)
                if 0 <= live(t, 3, S):
                    act.wait_ge(scattered2, t - 3 + 1)
                    if not early(t - 3, 1):
                        act.wait_ge(wsum_added, t - 3)
                    A.activation(wtile[:], mm[:, 1, 0:WIN * YW], ACT.Copy).then_inc(wtile_out, 1)

            def front2(s, k):
                def copy(q):
                    act.wait_ge(xt_pe, s * Q + q + 1)
                    if not (early(s, 1) and q < 2):
                        act.wait_ge(h_pe, s * Q + q - 1)
                    A.activation(x_t[:, q % 2, 0:QC * EP], tp[0:2 * D, q % 2, 0:QC * EP], ACT.Copy).then_inc(xt_out, 1)

                def relu(q):
                    act.wait_ge(h_pe, s * Q + q + 1)
                    if not (early(s, 1) and q < 2):
                        act.wait_ge(v_pe, s * Q + q - 1)
                    A.activation(h[:, q % 2, 0:QC * EP], mm[:, q % 2, 0:QC * EP], ACT.Relu,
                                 bias=bias1[:, 0:1]).then_inc(h_out, 1)

                copy(0)
                copy(1)
                relu(0)
                copy(2)
                relu(1)
                copy(3)
                relu(2)
                relu(3)

            def out_messages_two(s, k):
                out_messages(s, k, 1)

            def none(s, k):
                pass

            def copy_sums(done, out_sem):
                act.wait_ge(done, 1)
                for bank in range(3):
                    A.activation(sums[:, bank, :], acc[:, bank, :], ACT.Copy).then_inc(out_sem, 1)

            def give_root(value):
                A.activation(root[:], value[:], ACT.Sqrt).then_inc(root_given, 1)

            def node_update():
                act.wait_ge(node_dve, 1)
                give_root(deg)
                act.wait_ge(node_pe, 1)
                A.activation(turned[:, 0, :], tp[:, 0, :], ACT.Copy).then_inc(node_act, 1)
                for n in range(UPD):
                    act.wait_ge(node_pe, 3 + (0 if n == 0 else 2 * n - 1))
                    if n >= 2:
                        act.wait_ge(node_pe, 3 + 2 * (n - 1))
                    w = min(4, 2 * (BLOCKS - 2 * n)) * P
                    A.activation(turned[:, n % 2, 0:w], tp[:, n % 2, 0:w], ACT.Copy).then_inc(node_act, 1)
                act.wait_ge(node_pe, 2 + 2 * UPD)
                A.activation(aggl[:, 0:BLOCKS, :].rearrange("p b d -> p (b d)"), mm[:, 1, 0:BLOCKS * D], ACT.Silu,
                             scale=float(D * D) ** -0.5).then_inc(node_act, 1)
                act.wait_ge(node_pe, 3 + 2 * UPD)
                A.activation(turned[:, 0, :], tp[:, 0, :], ACT.Copy).then_inc(node_act, 1)
                act.wait_ge(root_asked, 1)
                give_root(stat)

            act.wait_ge(near_known, 1)
            is_near = act.value_load(near_i[0:1, 0:1], min_val=0, max_val=1)
            with act.If(is_near == 1):
                act.wait_ge(tab_made, 1)
                run_steps(act, S, near_first, 3)
                copy_sums(acc_done, sums_out)
                act.wait_ge(cnt_pe, 1)
                A.activation(counts_t[:], tp[0:S * WIN, 1, 0:P], ACT.Copy).then_inc(cnt_out, 1)
                node_update()
                act.wait_ge(tab_made, 2)
                run_steps(act, S, near_second, 3)
                copy_sums(acc2_done, sums2_out)
            with act.Else():
                run_tiles(act, S, out_messages_two, none)
                copy_sums(acc_done, sums_out)
                node_update()
                run_tiles(act, S, front2, none)
                copy_sums(acc2_done, sums2_out)
            act.wait_ge(root_asked, 2)
            give_root(stat)

        @block.vector
        def _(dve):
            V = nc.vector
            ch = Chain(dve, setup)
            link = ch.link
            V.memset(zeros[:], 0.0)
            V.memset(xn[:], 0.0)
            V.memset(agg[:], 0.0)
            V.memset(aggl[:], 0.0)
            V.memset(bd_msg[:], 0.0)
            V.memset(bd_upd[:], 0.0)
            V.memset(w2[:], 0.0)
            V.memset(ones_row[:], 1.0)
            V.memset(rows_tab[:], 0.0)
            link(V.memset(parts[:], 1.0))
            dve.wait_ge(iota_made, 3)
            link(V.tensor_copy(part_id[:], iota_p[:]))
            link(V.tensor_scalar(ident[:], iota_n[:, 0:P], part_id[:, 0:1], None, ALU.is_equal))
            V.tensor_scalar(part_id[:], part_id[:], 1.0, None, ALU.mult).then_inc(consts_ready, 1)
            dve.wait_ge(consts_ready, 1)
            dve.wait_ge(idx_in, 48)
            V.tensor_copy(dst_short[:], dst_int).then_inc(dst16_made, 1)

            def place(which):
                link(V.tensor_copy(fidx, idx[which][:]))
                link(V.tensor_scalar(span, fidx, float(NT), None, ALU.is_ge))
                for a in range(2, NA):
                    link(V.scalar_tensor_tensor(out=span, in0=fidx, scalar=float(NT * a), in1=span,
                                                op0=ALU.is_ge, op1=ALU.add))
                link(V.scalar_tensor_tensor(out=within[which][:], in0=span, scalar=-float(NT), in1=fidx,
                                            op0=ALU.mult, op1=ALU.add))
                for twice in range(2):
                    ins = V.tensor_tensor(in_span[which][:, :, :, twice],
                                          bcast(iota_n[0:EP, 0:NA].unsqueeze(1), (EP, C, NA)),
                                          bcast(span.unsqueeze(2), (EP, C, NA)), ALU.is_equal)
                link(ins)

            link(V.tensor_copy(fidx, idx[1][:]))
            tiles_of = fidx.rearrange("p (s c) -> p s c", c=CH)
            link(V.tensor_reduce(ends[:, 0, :], tiles_of, AX, ALU.min))
            link(V.tensor_reduce(ends[:, 1, :], tiles_of, AX, ALU.max))
            V.tensor_scalar(ends[:, 1, :], ends[:, 1, :], -1.0, None, ALU.mult).then_inc(ends_dve, 1)
            dve.wait_ge(ends_pe, 1)
            V.tensor_reduce(end_col[:], tp[0:2 * S, 0, 0:EP], AX, ALU.min).then_inc(ends_dve, 1)
            dve.wait_ge(ends_pe, 2)
            link(V.tensor_copy(end_row[:].rearrange("p t s -> p (t s)"), tp[0:1, 1, 0:2 * S]))
            link(V.tensor_tensor(passed, bcast(end_row[:, 0, :].unsqueeze(2), (1, S, BLOCKS - 1)),
                                 bcast(block_start[:].unsqueeze(1), (1, S, BLOCKS - 1)), ALU.is_ge))
            link(V.tensor_reduce(base[:], passed, AX, ALU.add))
            link(V.tensor_copy(base_i[:], base[:]))
            link(V.scalar_tensor_tensor(out=near_row[:], in0=base[:], scalar=float(P), in1=end_row[:, 1, :],
                                        op0=ALU.mult, op1=ALU.add))
            link(V.tensor_scalar(near_row[:], near_row[:], -float(WIN * P), None, ALU.is_gt))
            link(V.tensor_reduce(near[:], near_row[:], AX, ALU.min))
            for w in range(WIN):
                ins = V.tensor_scalar(base_row[:, :, w], base[:], float(w), None, ALU.add)
            ins.then_inc(ends_dve, 1)
            dve.wait_ge(ends_dve, 3)
            V.tensor_copy(near_i[:], near[:]).then_inc(near_known, 1)
            dve.wait_ge(ends_pe, 3)
            link(V.tensor_scalar(window[:].rearrange("p s w -> p (s w)"), mm[:, 0, 0:S * WIN], float(P), None,
                                 ALU.mult))
            link(V.tensor_tensor(within[1][:].rearrange("p (s c) -> p s c", c=CH), tiles_of,
                                 bcast(window[0:EP, :, 0].unsqueeze(2), (EP, S, CH)), ALU.subtract))
            link(V.tensor_scalar(window[:].rearrange("p s w -> p (s w)"), window[:].rearrange("p s w -> p (s w)"),
                                 part_id[:, 0:1], None, ALU.add))
            link(V.tensor_copy(base_col[:], mm[0:S * WIN, 1, 0:1]))
            link(V.tensor_scalar(select[:], iota_n[0:S * WIN, 0:BLOCKS], base_col[:, 0:1], None, ALU.is_equal))
            place(0)

            schain = Chain(dve, split_chain, 4)
            wchain = Chain(dve, split2_chain, 5)
            nch = Chain(dve, node_chain)
            nl = nch.link

            def split_messages(s, k):
                schain.step(s)
                dve.wait_ge(msg_made, s + 1)
                m = msg[:, k].rearrange("p c t d -> p (c t d)")[:, 0:CH * D].rearrange("p (c d) -> p c d", c=CH)
                rst = rest[:].rearrange("p c t d -> p (c t d)")[:, 0:CH * D].rearrange("p (c d) -> p c d", c=CH)
                if not early(s, 1):
                    dve.wait_ge(prod_made, s)
                schain.link(V.tensor_copy(parts[:, :, 0:D], m))
                schain.link(V.tensor_tensor(rst, m, parts[:, :, 0:D], ALU.subtract))
                schain.link(V.tensor_copy(parts[:, :, D:2 * D], rst))
                schain.link(V.tensor_tensor(rst, rst, parts[:, :, D:2 * D], ALU.subtract))
                V.tensor_copy(parts[:, :, 2 * D:3 * D], rst).then_inc(part_made, 1)
                dve.wait_ge(part_made, s + 1)

            def spread(target, which, s, source, width):
                full = (EP, CH, NA, width // 2, 2)
                return V.tensor_tensor(
                    target.rearrange("p c a (m t) -> p c a m t", t=2),
                    bcast(source.rearrange("p c (m t) -> p c m t", t=2).unsqueeze(2), full),
                    bcast(in_span[which][:, bass.ds(s * CH, CH), :, :].unsqueeze(3), full), ALU.mult)

            def make_outer(s, k):
                if not early(s, 2):
                    dve.wait_ge(turned_pe, (s - 1) * Q)
                V.tensor_tensor(outer[:, k], bcast(xj[:, k].unsqueeze(3), (EP, CH, D, DE)),
                                bcast(attr[:, k].unsqueeze(2), (EP, CH, D, DE)), ALU.mult).then_inc(outer_made, 1)

            def turned_onehots(s, k, arrived, picked, made):
                dve.wait_ge(arrived[k], landed(s, k, 1))
                if not early(s, 2):
                    dve.wait_ge(picked, 2 * (s - 1))
                    if made is hot_t_made:
                        dve.wait_ge(counted, WIN * (s - 1))
                for w in range(WIN):
                    V.tensor_scalar(hot_t[:, k, w, :], dst_all[:, k, :], window[:, bass.ds(s, 1), w], None,
                                    ALU.is_equal).then_inc(made, 1)

            def source_onehots(s, k, made):
                for c in range(CH):
                    ins = V.tensor_scalar(hots[:, k, c, :], iota_n[0:EP, :], within[0][:, bass.ds(s * CH + c, 1)],
                                          None, ALU.is_equal)
                ins.then_inc(made, 1)

            xchain = Chain(dve, xj_chain, 1)
            rchain = Chain(dve, rows_chain, 3)

            def near_first(t, r):
                if 0 <= live(t, 1, S):
                    s, k = t - 1, (r - 1) % 2
                    xchain.step(s)
                    dve.wait_ge(attr_in[k], landed(s, k, 1))
                    dve.wait_ge(picked_out, 2 * (s + 1))
                    p = picked[:].rearrange("p c t r -> p (c t r)")[:, 0:CH * PARTS * D].rearrange(
                        "p (c t d) -> p c t d", c=CH, t=PARTS)
                    if not early(s, 2):
                        dve.wait_ge(outer_made, s - 1)
                    xchain.link(V.tensor_tensor(xj[:, k], p[:, :, 0, :], p[:, :, 1, :], ALU.add))
                    V.tensor_tensor(xj[:, k], xj[:, k], p[:, :, 2, :], ALU.add).then_inc(xj_made, 1)
                    dve.wait_ge(xj_made, s + 1)
                    make_outer(s, k)
                if 0 <= live(t, 0, S):
                    turned_onehots(t, r % 2, dst_in, picked_pe, hot_t_made)
                if 0 <= live(t, 2, S):
                    s, k = t - 2, (r - 2) % 2
                    split_messages(s, k)
                    if not early(s, 2):
                        dve.wait_ge(scattered, s - 1)
                    spread(prod[:, k], 0, s, parts[:], MW).then_inc(prod_made, 1)
                    source_onehots(s, k, hots_made)

            full = (EP, CH, 2, D)
            hchain = Chain(dve, house_chain, 13)

            def take_vectors(s):
                V.tensor_tensor(v, vv[0:EP, :].rearrange("p (c t d) -> p c t d", c=CH, t=2),
                                bcast(bias2[:].unsqueeze(1), full), ALU.add).then_inc(v_out, 1)
                dve.wait_ge(v_out, s + 1)

            def reflect(s, k, slot):
                hchain.step(s)
                lk = hchain.link
                z = gath[:, slot][:, :, 0:4:3, :]
                m = msg[:, k]
                lk(V.tensor_tensor(sq[:], v, v, ALU.mult))
                lk(V.tensor_reduce(rnorm[:], sq[:], AX, ALU.add))
                lk(V.tensor_scalar(rnorm[:], rnorm[:], UNIT_FLOOR ** 2, 0.5, ALU.max, ALU.mult))
                lk(V.reciprocal(rnorm[:], rnorm[:]))
                lk(V.tensor_tensor(sq[:], v, z, ALU.mult))
                lk(V.tensor_reduce(scal[:], sq[:], AX, ALU.add))
                lk(V.tensor_tensor(scal[:], scal[:], rnorm[:], ALU.mult))
                lk(V.tensor_tensor(sq[:], v, bcast(scal[:].unsqueeze(3), full), ALU.mult))
                lk(V.tensor_tensor(t1[:], z, sq[:], ALU.subtract))
                for w in range(2):
                    ins = V.tensor_tensor(sq[:, :, w, :], v[:, :, w, :], t1[:, :, 1 - w, :], ALU.mult)
                lk(ins)
                lk(V.tensor_reduce(scal[:], sq[:], AX, ALU.add))
                lk(V.tensor_tensor(scal[:], scal[:], rnorm[:], ALU.mult))
                lk(V.tensor_tensor(sq[:], v, bcast(scal[:].unsqueeze(3), full), ALU.mult))
                for w in range(2):
                    ins = V.tensor_tensor(m[:, :, w, :], t1[:, :, 1 - w, :], sq[:, :, w, :], ALU.subtract)
                ins.then_inc(msg2_made, 1)
                dve.wait_ge(msg2_made, s + 1)

            def split_both(s, k):
                wchain.step(s)
                lk = wchain.link
                m = msg[:, k]

                def part(i):
                    return parts2[:, k, :, :, i * D:(i + 1) * D].rearrange("p w c d -> p c w d")

                lk(V.tensor_copy(part(0), m))
                lk(V.tensor_tensor(rest[:], m, part(0), ALU.subtract))
                lk(V.tensor_copy(part(1), rest[:]))
                lk(V.tensor_tensor(rest[:], rest[:], part(1), ALU.subtract))
                lk(V.tensor_copy(part(2), rest[:]))

            def near_second(t, r):
                if 0 <= live(t, 2, S):
                    dve.wait_ge(v_pe, (t - 2 + 1) * Q)
                    take_vectors(t - 2)
                if 0 <= live(t, 1, S):
                    s, slot = t - 1, (r - 1) % 4
                    rchain.step(s)
                    dve.wait_ge(picked2_out, 2 * (s + 1))
                    if not early(s, 4):
                        dve.wait_ge(msg2_made, s - 3)
                    x_d = gath[:, slot, :, 2, :]
                    rchain.link(V.tensor_tensor(picked[:, :, 0, :], picked[:, :, 0, :], picked[:, :, 1, :], ALU.add))
                    V.tensor_tensor(dis_e[:].unsqueeze(2), picked[:, :, 0, D:RW], picked[:, :, 2, D:RW], ALU.add)
                    rchain.link(V.tensor_tensor(x_d, picked[:, :, 0, 0:D], picked[:, :, 2, 0:D], ALU.add))
                    rchain.link(V.tensor_tensor(gath[:, slot, :, 3, :], x_d, bcast(dis_e[:].unsqueeze(2), (EP, CH, D)),
                                                ALU.mult))
                    V.tensor_copy(stat[0:1, 0:1], stat[0:1, 0:1]).then_inc(rows_made, 1)
                if 0 <= live(t, 0, S):
                    turned_onehots(t, r % 2, dst2_in, picked2_pe, hot_t2_made)
                if 0 <= live(t, 4, S):
                    s = t - 4
                    dve.wait_ge(wtile_out, s + 1)
                    first = dve.value_load(base_i[0:1, bass.ds(s, 1)], min_val=0, max_val=BLOCKS - 1)
                    there = wsum[:, bass.ds(first, WIN), :]
                    V.tensor_tensor(there, there, wtile[:].rearrange("p (w m) -> p w m", w=WIN),
                                    ALU.add).then_inc(wsum_added, 1)
                if 0 <= live(t, 2, S):
                    s, k = t - 2, (r - 2) % 2
                    dve.wait_ge(near_rows[(r - 2) % 4], landed(s, (r - 2) % 4, CH, 4))
                    reflect(s, k, (r - 2) % 4)
                    if not early(s, 2):
                        dve.wait_ge(scattered2, s - 1)
                    split_both(s, k)
                    spread(prod2[:, k], 0, s, parts2[:, k, 0], YW).then_inc(prod2_made, 1)
                    for c in range(CH):
                        V.tensor_scalar(win_hot[:, k, c, :], iota_n[0:EP, 0:WIN * P],
                                        within[1][:, bass.ds(s * CH + c, 1)], None, ALU.is_equal)
                    source_onehots(s, k, hots2_made)

            def front(s, k):
                dve.wait_ge(attr_in[k], landed(s, k, 1))
                dve.wait_ge(rows_in[k], landed(s, k, CH))
                make_outer(s, k)

            def back(s, k):
                split_messages(s, k)
                if not early(s, 2):
                    dve.wait_ge(hot_used, (s - 1) * CH)
                spread(prod[:, k], 0, s, parts[:], MW).then_inc(prod_made, 1)
                for c in range(CH):
                    if not (early(s, 1) and c < 4):
                        dve.wait_ge(hot_used, s * CH + c - 3)
                    V.tensor_scalar(dhot[:, c % 4, :], iota_n[0:EP, :], within[1][:, bass.ds(s * CH + c, 1)], None,
                                    ALU.is_equal)
                    V.tensor_scalar(hot[:, c % 4, :], iota_n[0:EP, :], within[0][:, bass.ds(s * CH + c, 1)], None,
                                    ALU.is_equal).then_inc(hot_made, 1)

            def nothing(s, k):
                pass

            def back2(s, k):
                dve.wait_ge(v_pe, (s + 1) * Q)
                take_vectors(s)
                dve.wait_ge(rows2_in[k], landed(s, k, 2 * CH))
                reflect(s, k, k)
                split_both(s, k)
                for w in range(2):
                    if not early(s, 1):
                        dve.wait_ge(hot2_used, (2 * s + w - 1) * CH)
                    spread(prod2[:, w], w, s, parts2[:, k, w], YW).then_inc(prod2_made, 1)
                    for c in range(CH):
                        if not (early(s, 1) and w == 0 and c < 4):
                            dve.wait_ge(hot2_used, (2 * s + w) * CH + c - 3)
                        V.tensor_scalar(hot[:, c % 4, :], iota_n[0:EP, :], within[w][:, bass.ds(s * CH + c, 1)], None,
                                        ALU.is_equal).then_inc(hot2_made, 1)

            def sum_parts(target, width):
                for b in range(NB):
                    cols = sums[:, b // 2, (b % 2) * NA * width:(b % 2 + 1) * NA * width].rearrange(
                        "p (a m) -> p a m", a=NA)
                    at = target[:, b:BLOCKS:NB, :]
                    nl(V.tensor_tensor(at, cols[:, :, 0:D], cols[:, :, D:2 * D], ALU.add))
                    nl(V.tensor_tensor(at, at, cols[:, :, 2 * D:3 * D], ALU.add))

            def inverse_root(value, target, turn):
                dve.wait_ge(root_given, turn)
                nl(V.reciprocal(target, root[:]))
                nl(V.tensor_tensor(newton[:], target, target, ALU.mult))
                nl(V.tensor_tensor(newton[:], newton[:], value, ALU.mult))
                nl(V.tensor_scalar(newton[:], newton[:], -0.5, 1.5, ALU.mult, ALU.add))
                nl(V.tensor_tensor(target, target, newton[:], ALU.mult))

            b3 = (P, BLOCKS, D)

            def layernorm(values, scratch, target, turn):
                nl(V.tensor_reduce(stat[:], values[:], AX, ALU.add))
                nl(V.tensor_scalar(stat[:], stat[:], 1.0 / D, None, ALU.mult))
                nl(V.tensor_tensor(values[:], values[:], bcast(stat[:].unsqueeze(2), b3), ALU.subtract))
                nl(V.tensor_tensor(scratch[:], values[:], values[:], ALU.mult))
                nl(V.tensor_reduce(stat[:], scratch[:], AX, ALU.add))
                V.tensor_scalar(stat[:], stat[:], 1.0 / D, NORM_EPS, ALU.mult, ALU.add).then_inc(root_asked, 1)
                dve.wait_ge(root_asked, turn - 1)
                inverse_root(stat[:], inv[:], turn)
                nl(V.tensor_tensor(target, values[:], bcast(inv[:].unsqueeze(2), b3), ALU.mult))

            def make_table(source, col, count):
                left = tmp2[:, :, 0:count]
                tab = rows_tab[:, 0:BLOCKS]
                nl(V.tensor_copy(tab[:, :, 0, col:col + count], source))
                nl(V.tensor_tensor(left, source, tab[:, :, 0, col:col + count], ALU.subtract))
                nl(V.tensor_copy(tab[:, :, 1, col:col + count], left))
                nl(V.tensor_tensor(left, left, tab[:, :, 1, col:col + count], ALU.subtract))
                nl(V.tensor_copy(tab[:, :, 2, col:col + count], left))

            def node_update(in_degree):
                dve.wait_ge(sums_out, 3)
                sum_parts(agg, MW)
                for b in range(NB):
                    cols = sums[:, b // 2, (b % 2) * GW:(b % 2 + 1) * GW].rearrange("p (a m) -> p a m", a=NA)
                    nl(V.tensor_tensor(deg[:, b:BLOCKS:NB].unsqueeze(2), cols[:, :, PARTS * D:PARTS * D + 1],
                                       in_degree(b), ALU.add))
                V.tensor_scalar(deg[:], deg[:], DEG_FLOOR, None, ALU.max).then_inc(node_dve, 1)
                dve.wait_ge(node_dve, 1)
                inverse_root(deg[:], dis[:], 1)
                dve.wait_ge(node_pe, 2)
                nl(V.tensor_scalar(aggl[:].rearrange("p b d -> p (b d)"), mm[:, 0, :], float(D) ** -0.5, None,
                                   ALU.mult))
                V.tensor_tensor(nouter, bcast(xn[:].unsqueeze(3), (P, BLOCKS, D, D)),
                                bcast(aggl[:, 0:BLOCKS, :].unsqueeze(2), (P, BLOCKS, D, D)),
                                ALU.mult).then_inc(node_dve, 1)
                dve.wait_ge(node_act, 2 + UPD)
                V.tensor_copy(stat[:], deg[:]).then_inc(node_dve, 1)
                dve.wait_ge(node_pe, 4 + 2 * UPD)
                nl(V.tensor_scalar(tmp[:].rearrange("p b d -> p (b d)"), mm[:, 0, 0:BLOCKS * D], float(D) ** -0.5,
                                   None, ALU.mult))
                nl(V.scalar_tensor_tensor(out=tmp[:], in0=xn[:], scalar=2.0, in1=tmp[:], op0=ALU.mult, op1=ALU.add))
                layernorm(tmp, tmp2, x1[:], 2)
                nl(V.tensor_copy(xz[:, :, D:2 * D], x1[:]))
                nl(V.tensor_tensor(xz[:, :, 0:D], x1[:], bcast(dis[:].unsqueeze(2), b3), ALU.mult))
                V.tensor_copy(xz[:, :, 2 * D:3 * D], xz[:, :, 0:D]).then_inc(table_ready, 1)

            def finish(extra):
                dve.wait_ge(sums2_out, 3)
                sum_parts(tmp2, YW)
                if extra:
                    for i in range(PARTS):
                        nl(V.tensor_tensor(tmp2[:], tmp2[:], wsum[:, 0:BLOCKS, i * D:(i + 1) * D], ALU.add))
                nl(V.tensor_tensor(tmp2[:], tmp2[:], bcast(dis[:].unsqueeze(2), b3), ALU.mult))
                nl(V.tensor_tensor(tmp2[:], tmp2[:], x1[:], ALU.add))
                nl(V.tensor_scalar(tmp2[:], tmp2[:], 0.0, None, ALU.max))
                nl(V.tensor_tensor(tmp[:], tmp2[:], x1[:], ALU.add))
                layernorm(tmp, tmp2, tmp[:], 3)
                V.tensor_copy(stat[:], deg[:]).then_inc(out_ready, 1)

            is_near = dve.value_load(near_i[0:1, 0:1], min_val=0, max_val=1)
            dve.wait_ge(nodes_in, 32)
            with dve.If(is_near == 1):
                tab = rows_tab[:].rearrange("p b t r -> p b (t r)")[:, 0:BLOCKS]
                nl(V.tensor_copy(tab[:, :, 0:D], xn[:]))
                nl(V.tensor_tensor(tmp2[:], xn[:], tab[:, :, 0:D], ALU.subtract))
                nl(V.tensor_copy(tab[:, :, D:2 * D], tmp2[:]))
                nl(V.tensor_tensor(tmp2[:], tmp2[:], tab[:, :, D:2 * D], ALU.subtract))
                V.tensor_copy(tab[:, :, 2 * D:3 * D], tmp2[:]).then_inc(tab_made, 1)
                run_steps(dve, S, near_first, 2)
                dve.wait_ge(counted, WIN * S)
                V.memset(wsum[:], 0.0).then_inc(cnt_out, 1)
                dve.wait_ge(cnt_out, 2)
                dve.wait_ge(cnt_pe, 2)
                node_update(lambda b: tp[:, 1, b:BLOCKS:NB].unsqueeze(2))
                make_table(x1[:], 0, D)
                make_table(dis[:].unsqueeze(2), D, 1)
                V.tensor_copy(stat[:], deg[:]).then_inc(tab_made, 1)
                run_steps(dve, S, near_second, 4)
                finish(True)
            with dve.Else():
                place(1)
                run_tiles(dve, S, front, back)
                node_update(lambda b: sums[:, 2, GW + b * NA:GW + (b + 1) * NA].unsqueeze(2))
                run_tiles(dve, S, nothing, back2)
                finish(False)


_INS = [("x", "x"), ("src", "src"), ("dst", "dst"), ("dst", "dst_flat"), ("edge_attr_8", "edge_attr"),
        ("L0_gnn_W_msg_tp", "w_msg_tp"), ("L0_gnn_W_msg_lin", "w_msg_lin"),
        ("L0_gnn_W_upd_tp", "w_upd_tp"), ("L0_gnn_W_upd_lin", "w_upd_lin"),
        ("L1_gnn_W1", "w1_t"), ("L1_gnn_b1", "b1"), ("L1_gnn_W2", "w2_t"), ("L1_gnn_b2", "b2")]


def kernel(**inputs):
    import numpy as np
    import concourse.bacc as bacc
    from concourse.bass_utils import run_bass_kernel_spmd

    nc = bacc.Bacc("TRN2", target_bir_lowering=False, num_devices=1)
    arrays, args = {}, []
    for given, name in _INS:
        a = np.asarray(inputs[given])
        if name in ("w1_t", "w2_t"):
            a = a.T
        elif name in ("src", "dst"):
            a = a.reshape(-1, EP).T
        elif name == "edge_attr":
            a = a.reshape(-1, CH, EP, a.shape[1]).transpose(0, 2, 1, 3).reshape(-1, EP, CH * a.shape[1])
        a = np.ascontiguousarray(a)
        arrays[name] = a
        args.append(nc.dram_tensor(name, a.shape, mybir.dt.from_np(a.dtype), kind="ExternalInput").ap())
    shape = inputs["x"].shape
    args.append(nc.dram_tensor("out", shape, F32, kind="ExternalOutput").ap())
    gnn_resnorm_kernel(nc, *args)
    r = run_bass_kernel_spmd(nc, [arrays], core_ids=[0])
    return r.results[0]["out"]
```

```python
from contextlib import ExitStack

import concourse.bass as bass
from concourse import mybir

ALU = mybir.AluOpType
ACT = mybir.ActivationFunctionType
F32 = mybir.dt.float32
BF16 = mybir.dt.bfloat16
F16 = mybir.dt.float16
I16 = mybir.dt.int16
I32 = mybir.dt.int32
AX = mybir.AxisListType.X

EP = 125
CH = 16
Q = 4
QC = CH // Q
P = 128
NB = 5
NA = 5
BLOCKS = NA * NB
WIN = 2
PADB = 32
LEAD = 6
STEPS = 4
PARTS = 3
PARTS2 = 2
Z_SCALE = 2.0 ** 13
NORM_EPS = 1e-5
DEG_FLOOR = 1e-5
UNIT_FLOOR = 1e-12


def bcast(ap, shape):
    return ap.broadcast_to(list(shape))


class Chain:

    def __init__(self, eng, sem, per_step=0):
        self.eng, self.sem, self.per, self.base, self.k = eng, sem, per_step, 0, 0

    def step(self, s):
        assert self.k in (0, self.per)
        self.base, self.k = s * self.per, 0

    def link(self, ins, between=None):
        self.k += 1
        ins.then_inc(self.sem, 1)
        if between is not None:
            between()
        self.eng.wait_ge(self.sem, self.base + self.k)


def run_tiles(eng, tiles, front, back):
    for s in range(3):
        front(s, s % 2)
        if s:
            back(s - 1, (s - 1) % 2)
    with eng.Fori(3, tiles - 2, 2) as i:
        front(i, 1)
        back(i - 1, 0)
        front(i + 1, 0)
        back(i, 1)
    front(tiles - 1, 1)
    back(tiles - 2, 0)
    back(tiles - 1, 1)


def run_steps(eng, tiles, step, depth):
    for t in range(LEAD):
        step(t, t)
    with eng.Fori(LEAD, tiles - STEPS + 1, STEPS) as i:
        for u in range(STEPS):
            step(i + u, LEAD + u)
    for t in range(tiles, tiles + depth):
        step(t, t)


def landed(s, k, dmas, slots=2):
    return s * (16 // slots * dmas) + (16 - 16 // slots * k) * dmas


def live(t, j, tiles):
    return -1 if isinstance(t, int) and not 0 <= t - j < tiles else 0


def early(s, n):
    return isinstance(s, int) and s < n


def gnn_resnorm_kernel(nc, x, src, dst, dst_flat, edge_attr, w_msg_tp, w_msg_lin, w_upd_tp, w_upd_lin,
                       w1_t, b1, w2_t, b2, out):
    N, D = x.shape
    E = dst_flat.shape[0]
    DE = edge_attr.shape[2] // CH
    HID = b1.shape[0]
    S = E // (EP * CH)
    C = S * CH
    FULLB, TAIL = N // P, N % P
    KM = D * DE
    MW = PARTS2 * D + 2
    TE = EP * CH
    RW = 2 * D
    HALF = CH // 2
    UPD = (BLOCKS + 1) // 2
    UPD_PIECE = 8
    GW = NA * MW
    XW = PARTS * D
    YW = PARTS2 * D
    YG = NA * YW
    NT = NB * P
    assert WIN == 2 and S * EP * CH == E and S % 2 == 0 and (S - LEAD) % STEPS == 0 and KM == P and BLOCKS * P >= N and 2 * HID == P

    with ExitStack() as ctx:
        def sb(name, shape, dt=F32):
            return ctx.enter_context(nc.sbuf_tensor(name, shape, dt))

        def ps(name, shape):
            return ctx.enter_context(nc.psum_tensor(name, shape, F32))

        def sem(name):
            return ctx.enter_context(nc.semaphore(name))

        table_s = nc.dram_tensor("table_s", (BLOCKS * P, 2 * D), F32, kind="Internal").ap()
        dst16 = nc.dram_tensor("dst16", (E,), I16, kind="Internal").ap()
        table_d = nc.dram_tensor("table_d", (BLOCKS * P, 2 * D), F32, kind="Internal").ap()

        acc = ps("acc", [P, 3, 512])
        tp = ps("tp", [P, 2, 512])
        mm = ps("mm", [P, 2, 512])
        vv = ps("vv", [P, 512])

        iota_n = sb("iota_n", [P, NT], I16)
        iota_p = sb("iota_p", [P, 1], I32)
        iota_twice = sb("iota_twice", [P, NA, 2], I16)
        part_id = sb("part_id", [P, 1])
        ident = sb("ident", [P, P])
        zeros = sb("zeros", [P, 512], BF16)
        w_msg = sb("w_msg", [P, D])
        w_upd = sb("w_upd", [P, 2, D])
        bd_msg = sb("bd_msg", [P, P])
        bd_upd = sb("bd_upd", [P, P])
        w1 = sb("w1", [P, 2, 2 * HID])
        w2 = sb("w2", [2 * HID, 2 * D])
        bias1 = sb("bias1", [2 * HID, 1])
        bias2 = sb("bias2", [PARTS, CH, 2, D])
        bias2_parts = sb("bias2_parts", [PARTS, CH, 2, D], BF16)
        ones_parts = sb("ones_parts", [PARTS, P], BF16)
        past_row = sb("past_row", [PARTS, 1])
        idx = [sb("src_idx", [EP, C + CH], I32), sb("dst_idx", [EP, C], I32)]
        idx_now = sb("idx_now", [EP, 4, 2, CH], I32)
        within = [sb("src_within", [EP, C]), sb("dst_within", [EP, C])]
        within_win = within[1][:].bitcast(I16).rearrange("p (c t) -> p c t", t=2)
        TEP = TE + 4
        near_or_span = sb("near_or_span", [P, 2 * WIN * TEP], BF16)
        hot_t = near_or_span[:].rearrange("p (k w e) -> p k w e", k=2, w=WIN)
        hot_t2 = near_or_span[:].bitcast(F16).rearrange("p (k w e) -> p k w e", k=2, w=WIN)
        in_span = [sb("src_in_span", [EP, C, NA, 2], BF16)[:],
                   near_or_span[0:EP, 0:C * NA * 2].rearrange("p (c a t) -> p c a t", a=NA, t=2)]
        xn = sb("xn", [P, BLOCKS, D])
        agg = sb("agg", [P, PADB, D])
        aggl = sb("aggl", [P, PADB, D])
        deg = sb("deg", [P, BLOCKS])
        dis = sb("dis", [P, BLOCKS])
        tmp = sb("tmp", [P, BLOCKS, D])
        tmp2 = sb("tmp2", [P, BLOCKS, D])
        stat = sb("stat", [P, BLOCKS])
        root = sb("root", [P, BLOCKS])
        inv = sb("inv", [P, BLOCKS])
        newton = sb("newton", [P, BLOCKS])
        x1 = sb("x1", [P, BLOCKS, D])
        xz = sb("xz", [P, BLOCKS, 3 * D])
        hot_space = sb("hot_space", [P, 2 * CH * NT], BF16)
        hots = hot_space[:].bitcast(F16)[0:EP, :].rearrange("p (k c n) -> p k c n", k=2, c=CH)
        space32 = hot_space[:].bitcast(F32)
        nouter = space32[:, 0:BLOCKS * D * D].rearrange("p (b i h) -> p b i h", b=BLOCKS, i=D)
        turned = space32[:, BLOCKS * D * D:BLOCKS * D * D + 1024].rearrange("p (t n) -> p t n", t=2)
        sums = space32[:, BLOCKS * D * D + 1024:BLOCKS * D * D + 1024 + 1536].rearrange("p (t n) -> p t n", t=3)
        fidx = space32[0:EP, 0:C]
        span = space32[0:EP, C:2 * C]
        span_twice = space32[0:EP, 2 * C:3 * C].bitcast(I16).rearrange("p (c t) -> p c t", t=2)
        dst_int = space32[0:EP, 2 * C:3 * C].bitcast(I32)
        attr_all = space32[0:EP, CH * NT - S * CH * DE:CH * NT]
        maxima = sb("maxima", [P, 3])
        minima = sb("minima", [P, 3])
        max_col = sb("max_col", [3, 1])
        bound = sb("bound", [1, 4])
        power = sb("power", [1, 2])
        scale_row = sb("scale_row", [1, 2])
        scale = sb("scale", [P, 2])
        dst_short = sb("dst_short", [EP, C], I16)
        ends = sb("ends", [EP, 2, S])
        end_col = sb("end_col", [2 * S, 1])
        end_row = sb("end_row", [1, 2, S])
        block_start = sb("block_start", [1, BLOCKS - 1], I16)
        passed = space32[0:1, 3 * C:3 * C + S * (BLOCKS - 1)].rearrange("p (s b) -> p s b", s=S)
        base = sb("base", [1, S])
        near_row = sb("near_row", [1, S])
        base_i = sb("base_i", [1, S + 1], I32)
        near = sb("near", [1, 1])
        near_i = sb("near_i", [1, 1], I32)
        base_row = sb("base_row", [1, S, WIN])
        ones_row = sb("ones_row", [1, P])
        base_col = sb("base_col", [S * WIN, 1])
        window = sb("window", [P, S, WIN])
        counts = sb("counts", [P, S, WIN])
        counts_t = sb("counts_t", [S * WIN, P])
        select = sb("select", [S * WIN, BLOCKS])
        dst_all = sb("dst_all", [P, 2, TE], I16)
        distance = sb("distance", [P, QC * EP], BF16)
        minus_node = sb("minus_node", [P, S])
        ones_col = sb("ones_col", [P, 1])
        rows_tab = sb("rows_tab", [P, BLOCKS + WIN - 1, max(XW, PARTS2 * RW)], BF16)
        rows_tab2 = rows_tab[:].bitcast(F16)
        win_tab = sb("win_tab", [P, 2, WIN, max(XW, PARTS2 * RW)], BF16)
        win_tab2 = win_tab[:].bitcast(F16)
        wsum = sb("wsum", [P, BLOCKS + WIN - 1, YW])
        wtile = sb("wtile", [P, WIN * YW])
        win_space = sb("win_space", [P, 2 * CH * WIN * P], BF16)
        win_hots = win_space[0:EP, :]
        count_junk = win_space[:, 0:TE]
        small_space = sb("small_space", [EP, 2 * CH * D + 2 * CH * DE + CH * PARTS * D])
        at_attr = 2 * CH * D
        at_picked = at_attr + 2 * CH * DE
        xj = small_space[:, 0:at_attr].rearrange("p (k c d) -> p k c d", k=2, c=CH)
        attr = small_space[:, at_attr:at_picked].rearrange("p (k c j) -> p k c j", k=2, c=CH)
        picked = small_space[:, at_picked:at_picked + CH * PARTS * D]
        v = small_space[:, 0:2 * CH * 2 * D].rearrange("p (k c t d) -> p k c t d", k=2, c=CH, t=2)
        t1 = small_space[:, 4 * CH * D:6 * CH * D].rearrange("p (c t d) -> p c t d", c=CH, t=2)
        edge_space = sb("edge_space", [EP, 2 * CH * D * DE])
        outer = edge_space[:].rearrange("p (k c i j) -> p k c i j", k=2, c=CH, i=D)
        gath = edge_space[:].rearrange("p (k c f d) -> p k c f d", k=4, c=CH, f=4)
        outer_t = sb("outer_t", [P, 2, 512])
        msg = sb("msg", [EP, 2, CH, 2, D])
        part_space = sb("part_space", [EP, max(2 * 2 * CH * YW, CH * MW)], BF16)
        parts = part_space[:].bitcast(F16)[:, 0:CH * MW].rearrange("p (c m) -> p c m", m=MW)
        parts2 = part_space[:].bitcast(F16)[:, 0:2 * 2 * CH * YW].rearrange("p (k w c m) -> p k w c m", k=2, w=2, c=CH)
        prod_space = sb("prod_space", [EP, 2 * CH * NA * MW], BF16)
        prod = prod_space[:].bitcast(F16).rearrange("p (k c a m) -> p k c a m", k=2, c=CH, a=NA)
        prod2 = prod_space[:].bitcast(F16)[:, 0:2 * CH * NA * YW].rearrange("p (k c a m) -> p k c a m", k=2, c=CH, a=NA)
        win_hot = win_hots.bitcast(F16)[:, 0:2 * CH * P].rearrange("p (k c n) -> p k c n", k=2, c=CH)
        in_block = win_hots.bitcast(F16)[:, 2 * CH * P:2 * CH * P + C * WIN * 2].rearrange(
            "p (c w t) -> p c w t", w=WIN, t=2)
        win_prod = sb("win_prod", [EP, 2, CH, WIN, YW], F16)
        hot = hots[:, 0]
        dhot = win_hots[:, 0:4 * NT].rearrange("p (c n) -> p c n", c=4)
        x_t = sb("x_t", [P, 2, 2 * EP])
        h = outer_t
        sq = agg[0:EP].rearrange("p (c w) d -> p c w d", c=CH)
        vsq = sb("vsq", [EP, 2, CH, 2, D])
        scal = sb("scal", [EP, CH, 2])
        rnorm = sb("rnorm", [EP, CH, 2])

        idx_in = sem("idx_in")
        nodes_in = sem("nodes_in")
        weights_in = sem("weights_in")
        iota_made = sem("iota_made")
        dst16_made = sem("dst16_made")
        dst16_out = sem("dst16_out")
        ends_dve = sem("ends_dve")
        ends_pe = sem("ends_pe")
        near_known = sem("near_known")
        dst_in = [sem("dst_in0"), sem("dst_in1")]
        dst2_in = [sem("dst2_in0"), sem("dst2_in1")]
        near_rows = [sem(f"near_rows{i}") for i in range(4)]
        tab_made = sem("tab_made")
        hot_t_made = sem("hot_t_made")
        win_tab_made = sem("win_tab_made")
        picked_pe = sem("picked_pe")
        picked_out = sem("picked_out")
        counted = sem("counted")
        xj_made = sem("xj_made")
        xj_chain = sem("xj_chain")
        scattered = sem("scattered")
        hots_made = sem("hots_made")
        cnt_pe = sem("cnt_pe")
        cnt_out = sem("cnt_out")
        hot_t2_made = sem("hot_t2_made")
        hot_t_act = sem("hot_t_act")
        distances = sem("distances")
        act_held = sem("act_held")
        win_tab2_made = sem("win_tab2_made")
        picked2_pe = sem("picked2_pe")
        picked2_out = sem("picked2_out")
        scattered2 = sem("scattered2")
        hots2_made = sem("hots2_made")
        wtile_out = sem("wtile_out")
        wsum_added = sem("wsum_added")
        setup = sem("setup")
        consts_ready = sem("consts_ready")
        root_asked = sem("root_asked")
        root_given = sem("root_given")
        pool_held = sem("pool_held")
        idx_placed = sem("idx_placed")
        idx2_placed = sem("idx2_placed")
        attr_in = [sem("attr_in0"), sem("attr_in1")]
        rows_in = [sem("rows_in0"), sem("rows_in1")]
        outer_made = sem("outer_made")
        turned_pe = sem("turned_pe")
        turned_out = sem("turned_out")
        msg_pe = sem("msg_pe")
        msg_made = sem("msg_made")
        part_made = sem("part_made")
        split_chain = sem("split_chain")
        prod_made = sem("prod_made")
        hot_made = sem("hot_made")
        hot_used = sem("hot_used")
        acc_zero = sem("acc_zero")
        acc_done = sem("acc_done")
        sums_out = sem("sums_out")
        node_pe = sem("node_pe")
        node_act = sem("node_act")
        node_dve = sem("node_dve")
        node_chain = sem("node_chain")
        table_ready = sem("table_ready")
        table_out = sem("table_out")
        rows2_in = [sem("rows2_in0"), sem("rows2_in1")]
        xt_pe = sem("xt_pe")
        xt_out = sem("xt_out")
        h_pe = sem("h_pe")
        attr_all_in = sem("attr_all_in")
        attr_abs = sem("attr_abs")
        bound_dve = sem("bound_dve")
        bound_pe = sem("bound_pe")
        h_out = sem("h_out")
        v_pe = sem("v_pe")
        v_out = sem("v_out")
        msg2_made = sem("msg2_made")
        rows_read = sem("rows_read")
        sources_placed = sem("sources_placed")
        house_chain = sem("house_chain")
        split2_chain = sem("split2_chain")
        prod2_made = sem("prod2_made")
        hot2_made = sem("hot2_made")
        hot2_used = sem("hot2_used")
        acc2_zero = sem("acc2_zero")
        acc2_done = sem("acc2_done")
        sums2_out = sem("sums2_out")
        out_ready = sem("out_ready")
        out_stored = sem("out_stored")

        x_lo = x[0:FULLB * P, :].rearrange("(h p) d -> p h d", p=P)
        out_lo = out[0:FULLB * P, :].rearrange("(h p) d -> p h d", p=P)
        N_WEIGHT_DMAS = 2 + 2 * 8 + 3 * 2 + 3 * 2

        block = ctx.enter_context(nc.Block())

        @block.sync
        def _(sp):
            sp.dma_start(idx[0][:, 0:C], src).then_inc(idx_in, 16)
            sp.dma_start(idx[1][:], dst).then_inc(idx_in, 16)
            sp.dma_start(dst_int, dst_flat.rearrange("(p k) -> p k", p=EP)).then_inc(idx_in, 16)

            sp.dma_start(attr_all.rearrange("p (s f) -> p s f", s=S),
                         edge_attr.rearrange("s p f -> p s f")).then_inc(attr_all_in, 16)

            def load_attr(s, k):
                sp.dma_start(attr[:, k].rearrange("p c j -> p (c j)"),
                             edge_attr[bass.ds(s, 1)].rearrange("o p f -> (o p) f")).then_inc(attr_in[k], 16)

            load_attr(0, 0)
            load_attr(1, 1)
            sp.wait_ge(consts_ready, 1)
            sp.dma_start(xn[:, 0:FULLB, :], x_lo).then_inc(nodes_in, 16)
            sp.dma_start(xn[0:TAIL, FULLB, :], x[FULLB * P:N, :]).then_inc(nodes_in, 16)
            sp.dma_start(w_msg[:], w_msg_tp.rearrange("i j h -> (i j) h")).then_inc(weights_in, 16)
            sp.dma_start(w_upd[:], w_upd_tp.rearrange("(t i) h k -> (i h) t k", t=2)).then_inc(weights_in, 16)
            for g in range(8):
                r = slice(g * D, (g + 1) * D)
                sp.dma_start(bd_msg[r, r], w_msg_lin).then_inc(weights_in, 16)
                sp.dma_start(bd_upd[r, r], w_upd_lin).then_inc(weights_in, 16)
            for j in range(2):
                r = 2 * RW * j + D
                sp.dma_start(w1[r:r + 2 * D, j, 0:HID], w1_t).then_inc(weights_in, 16)
                sp.dma_start(w1[r:r + D, j, HID:2 * HID], w1_t[D:2 * D, :]).then_inc(weights_in, 16)
                sp.dma_start(w1[r + D:r + 2 * D, j, HID:2 * HID], w1_t[0:D, :]).then_inc(weights_in, 16)
            for g in range(2):
                sp.dma_start(w2[g * HID:(g + 1) * HID, g * D:(g + 1) * D], w2_t).then_inc(weights_in, 16)
                sp.dma_start(bias1[g * HID:(g + 1) * HID, :], b1.unsqueeze(1)).then_inc(weights_in, 16)
                sp.dma_start(bias2[:, :, g, :], bcast(b2.unsqueeze(0).unsqueeze(0), (PARTS, CH, D))).then_inc(weights_in, 16)
            sp.wait_ge(dst16_made, 1)
            sp.dma_start(dst16.rearrange("(p k) -> p k", p=EP), dst_short[:]).then_inc(dst16_out, 16)
            sp.wait_ge(dst16_out, 16)

            def load_dst(s, k, landed_in):
                sp.dma_start(dst_all[:, k, :],
                             bcast(dst16.rearrange("(s e) -> s e", s=S)[bass.ds(s, 1), :], (P, TE))).then_inc(landed_in[k], 16)

            sp.wait_ge(near_known, 1)
            is_near = sp.value_load(near_i[0:1, 0:1], min_val=0, max_val=1)
            with sp.If(is_near == 1):
                load_dst(0, 0, dst_in)
                load_dst(1, 1, dst_in)
                with sp.Fori(2, S - 1, 2) as i:
                    for k in range(2):
                        sp.wait_ge(hot_t_made, WIN * (i + k - 1))
                        load_dst(i + k, k, dst_in)
                        sp.wait_ge(outer_made, i + k - 1)
                        load_attr(i + k, k)
                sp.wait_ge(hot_t_made, WIN * S)
                load_dst(0, 0, dst2_in)
                load_dst(1, 1, dst2_in)
                sp.wait_ge(table_ready, 1)
                sp.dma_start(table_s.rearrange("(h p) f -> p h f", p=P), xz[:, :, 0:2 * D]).then_inc(table_out, 16)
                with sp.Fori(2, S - 1, 2) as i:
                    for k in range(2):
                        sp.wait_ge(picked2_pe, i + k - 1)
                        load_dst(i + k, k, dst2_in)
            with sp.Else():
                with sp.Fori(2, S - 1, 2) as i:
                    for k in range(2):
                        sp.wait_ge(outer_made, i + k - 1)
                        load_attr(i + k, k)
                sp.wait_ge(table_ready, 2)
                sp.dma_start(table_s.rearrange("(h p) f -> p h f", p=P), xz[:, :, 0:2 * D]).then_inc(table_out, 16)
                sp.dma_start(table_d.rearrange("(h p) f -> p h f", p=P), xz[:, :, D:3 * D]).then_inc(table_out, 16)
            sp.wait_ge(out_ready, 1)
            sp.dma_start(out_lo, tmp[:, 0:FULLB, :]).then_inc(out_stored, 16)
            sp.dma_start(out[FULLB * P:N, :], tmp[0:TAIL, FULLB, :]).then_inc(out_stored, 16)
            sp.wait_ge(out_stored, 32)

        @block.gpsimd
        def _(pool):
            nc.gpsimd.iota(iota_n[:], [[1, NT]], base=0, channel_multiplier=0).then_inc(iota_made, 1)
            nc.gpsimd.iota(iota_p[:], [[0, 1]], base=0, channel_multiplier=1).then_inc(iota_made, 1)
            nc.gpsimd.iota(iota_twice[:], [[1, NA], [0, 2]], base=0, channel_multiplier=0).then_inc(iota_made, 1)
            nc.gpsimd.iota(block_start[:], [[P, BLOCKS - 1]], base=P, channel_multiplier=0).then_inc(iota_made, 1)
            pool.wait_ge(idx_in, 48)

            def hold(signal, count):
                pool.wait_ge(signal, count)
                pool.sem_inc(pool_held, 1)

            def gather(rows, table, which, k, c, signal):
                nc.gpsimd.indirect_dma_start(
                    rows, None, table, bass.IndirectOffsetOnAxis(ap=idx_now[:, k, which, c:c + 1], axis=0)
                ).then_inc(signal, 16)

            def place_indices(which, s, k, copied, count):
                nc.gpsimd.tensor_copy(idx_now[:, k, which, :],
                                      idx[which][:, bass.ds(s * CH, CH)]).then_inc(copied, 1)
                hold(copied, count)

            def first_rows(s, k):
                if not early(s, 2):
                    hold(outer_made, s - 1)
                place_indices(1, s, k, idx_placed, s + 1)
                for c in range(CH):
                    gather(xj[:, k, c, :], x, 1, k, c, rows_in[k])

            def second_rows(s, k):
                if not early(s, 2):
                    hold(rows_read, s - 1)
                place_indices(0, s, k, idx2_placed, s * 2 + 1)
                place_indices(1, s, k, idx2_placed, s * 2 + 2)
                for c in range(CH):
                    gather(gath[:, k, c, 0:2, :].rearrange("p a d -> p (a d)"), table_s, 0, k, c, rows2_in[k])
                    gather(gath[:, k, c, 2:4, :].rearrange("p a d -> p (a d)"), table_d, 1, k, c, rows2_in[k])

            def source_rows(s, r):
                if not early(s, 4):
                    hold(sources_placed, s - 2)
                for c in range(CH):
                    gather(gath[:, r, c, 0:2, :].rearrange("p a d -> p (a d)"), table_s, 0, r, c, near_rows[r])

            pool.wait_ge(near_known, 1)
            is_near = pool.value_load(near_i[0:1, 0:1], min_val=0, max_val=1)
            with pool.If(is_near == 1):
                pool.wait_ge(sources_placed, 1)
                pool.wait_ge(table_out, 16)
                for s in range(LEAD):
                    source_rows(s, s % 4)
                with pool.Fori(LEAD, S - STEPS + 1, STEPS) as i:
                    for u in range(STEPS):
                        source_rows(i + u, (LEAD + u) % 4)
            with pool.Else():
                first_rows(0, 0)
                first_rows(1, 1)
                with pool.Fori(2, S - 1, 2) as i:
                    first_rows(i, 0)
                    first_rows(i + 1, 1)
                pool.wait_ge(table_out, 32)
                second_rows(0, 0)
                second_rows(1, 1)
                with pool.Fori(2, S - 1, 2) as i:
                    second_rows(i, 0)
                    second_rows(i + 1, 1)

        @block.tensor
        def _(pe):
            T = nc.tensor

            def clear_acc(done):
                for bank in range(3):
                    ins = T.matmul(acc[:, bank, :], zeros[:, 0:P], zeros[:], start=True, stop=False,
                                   skip_group_check=True)
                ins.then_inc(done, 1)

            def find_windows():
                pe.wait_ge(ends_dve, 1)
                T.transpose(tp[0:2 * S, 0, 0:EP], ends[:].rearrange("p t s -> p (t s)"),
                            ident[0:EP, 0:EP]).then_inc(ends_pe, 1)
                pe.wait_ge(ends_dve, 2)
                T.transpose(tp[0:1, 1, 0:2 * S], end_col[:], ident[0:2 * S, 0:2 * S]).then_inc(ends_pe, 1)
                pe.wait_ge(ends_dve, 3)
                row = base_row[:].rearrange("p s w -> p (s w)")
                T.matmul(mm[:, 0, 0:S * WIN], ones_row[:], row, start=True, stop=True)
                T.transpose(mm[0:S * WIN, 1, 0:1], row, ident[0:1, 0:1]).then_inc(ends_pe, 1)

            def find_bound():
                at = CH * D
                pe.wait_ge(bound_dve, 1)
                T.transpose(mm[0:3, 0, at:at + P], maxima[:], ident[:]).then_inc(bound_pe, 1)
                pe.wait_ge(bound_dve, 2)
                T.transpose(mm[0:1, 0, at + P:at + P + 3], max_col[:], ident[0:3, 0:3]).then_inc(bound_pe, 1)
                pe.wait_ge(bound_dve, 3)
                T.matmul(mm[:, 0, at + P + 4:at + P + 6], ones_row[:], scale_row[:], start=True,
                         stop=True).then_inc(bound_pe, 1)
                pe.wait_ge(bound_dve, 4)

            def turn(s, k, q):
                if q == 0:
                    pe.wait_ge(outer_made, s + 1)
                if not (early(s, 1) and q < 2):
                    pe.wait_ge(turned_out, s * Q + q - 1)
                for j in range(QC):
                    ins = T.transpose(tp[:, q % 2, j * EP:(j + 1) * EP],
                                      outer[:, k, q * QC + j].rearrange("p i j -> p (i j)"), ident[0:EP, 0:EP])
                ins.then_inc(turned_pe, 1)

            def messages(s, k, q, slot):
                pe.wait_ge(turned_out, s * Q + q + 1)
                if q == 0 and not early(s, 1 + slot):
                    pe.wait_ge(msg_made, s - slot)
                for j in range(QC):
                    c = q * QC + j
                    ins = T.matmul(mm[0:EP, k * slot, c * D:(c + 1) * D], outer_t[:, q % 2, j * EP:(j + 1) * EP],
                                   w_msg[:], start=True, stop=True)
                ins.then_inc(msg_pe, 1)

            def pick(s, k, half, bank, onehots, tables, out_sem, done):
                if half == 0:
                    pe.wait_ge(onehots, WIN * (s + 1))
                    pe.wait_ge(tables, s + 1)
                if not early(s, 1):
                    pe.wait_ge(out_sem, 2 * s + half - 1)
                for c in range(half * HALF, (half + 1) * HALF):
                    for w in range(WIN):
                        ins = T.matmul(bank[:, (c % HALF) * XW:(c % HALF + 1) * XW],
                                       hot_t[:, k, w, c * EP:c * EP + P],
                                       win_tab[:, k, w, 0:XW], start=(w == 0), stop=(w == WIN - 1))
                ins.then_inc(done, 1)

            def pick_sum(s, k, half):
                if half == 0:
                    pe.wait_ge(hot_t2_made, (WIN - 1) * (s + 1))
                    pe.wait_ge(hot_t_act, Q * (s + 1))
                    pe.wait_ge(win_tab2_made, s + 1)
                    if not early(s, 1):
                        pe.wait_ge(picked2_out, s)
                for c in range(half * HALF, (half + 1) * HALF):
                    for w in range(WIN):
                        for i in range(PARTS2):
                            ins = T.matmul(tp[:, 1, c * RW:(c + 1) * RW],
                                           hot_t2[:, k, w, c * EP:c * EP + P],
                                           win_tab2[:, k, w, i * RW:(i + 1) * RW],
                                           start=(w == 0 and i == 0), stop=(w == WIN - 1 and i == PARTS2 - 1))
                if half == 1:
                    ins.then_inc(picked2_pe, 1)

            def add_sources(s, k, chunks, onehot, products, made, onehots, done):
                if chunks.start == 0:
                    pe.wait_ge(made, s + 1)
                    pe.wait_ge(onehots, s + 1)
                width = NA * products.shape[-1]
                for c in chunks:
                    for b in range(NB):
                        ins = T.matmul(acc[:, b // 2, (b % 2) * width:(b % 2) * width + width],
                                       onehot[:, k, c, b * P:(b + 1) * P],
                                       products[:, k, c].rearrange("p a m -> p (a m)"),
                                       start=False, stop=False, skip_group_check=True)
                if chunks.stop == CH and done is not None:
                    ins.then_inc(done, 1)

            def near_first(t, r):
                def turn_if(q):
                    if 0 <= live(t, 2, S):
                        turn(t - 2, (r - 2) % 2, q)

                def msg_if(q):
                    if 0 <= live(t, 2, S):
                        messages(t - 2, (r - 2) % 2, q, 0)

                def pick_if(half):
                    if 0 <= live(t, 0, S):
                        pick(t, r % 2, half, (mm[:, 1, :], vv)[half], hot_t_made, win_tab_made,
                             picked_out, picked_pe)

                def add_if(first, last):
                    if 0 <= live(t, 4, S):
                        add_sources(t - 4, (r - 4) % 2, range(first, last), hots, prod, prod_made, hots_made, scattered)

                turn_if(0)
                add_if(0, 2)
                turn_if(1)
                add_if(2, 4)
                pick_if(0)
                msg_if(0)
                add_if(4, 5)
                turn_if(2)
                add_if(5, 7)
                pick_if(1)
                msg_if(1)
                add_if(7, 8)
                turn_if(3)
                add_if(8, 10)
                msg_if(2)
                add_if(10, 13)
                msg_if(3)
                add_if(13, 16)
                if isinstance(t, int) and t == 2:
                    pe.wait_ge(msg_made, 1)
                    find_bound()

            def layer_rows(s, slot, q, banks, arrived):
                if q == 0:
                    arrived()
                if not (early(s, 1) and q < banks):
                    pe.wait_ge(xt_out, s * Q + q - (banks - 1))
                for j in range(2):
                    c = q * QC + 2 * j
                    ins = T.transpose(tp[:, q % banks, j * EP:(j + 1) * EP],
                                      gath[:, slot, c:c + 2].rearrange("p c f d -> p (c f d)"), ident[0:EP, 0:EP])
                ins.then_inc(xt_pe, 1)

            def hidden(s, q, banks):
                pe.wait_ge(xt_out, s * Q + q + 1)
                if not (early(s, 1) and q < banks):
                    pe.wait_ge(h_out, s * Q + q - (banks - 1))
                for j in range(QC):
                    ins = T.matmul(mm[:, q % banks, j * EP:(j + 1) * EP], w1[:, j % 2, :],
                                    x_t[:, q % 2, (j // 2) * EP:(j // 2 + 1) * EP],
                                   start=True, stop=True)
                ins.then_inc(h_pe, 1)

            def vectors(s, q):
                pe.wait_ge(h_out, s * Q + q + 1)
                if q == 0:
                    if not early(s, 1):
                        pe.wait_ge(v_out, 2 * s)
                    T.matmul(vv[:, :], ones_parts[:], bias2_parts[:].rearrange("p c t d -> p (c t d)"),
                             start=True, stop=False, skip_group_check=True)
                for j in range(QC):
                    c = q * QC + j
                    ins = T.matmul(vv[0:EP, c * 2 * D:(c + 1) * 2 * D], h[:, q % 2, j * EP:(j + 1) * EP],
                                   w2[:], start=False, stop=False, skip_group_check=True)
                ins.then_inc(v_pe, 1)

            def near_second(t, r):
                s = t - 2

                def arrived():
                    pe.wait_ge(near_rows[(r - 2) % 4], landed(s, (r - 2) % 4, CH, 4))
                    pe.wait_ge(picked2_out, s + 1)

                def rows_if(q):
                    if 0 <= live(t, 2, S):
                        layer_rows(s, (r - 2) % 4, q, 1, arrived)

                def hidden_if(q):
                    if 0 <= live(t, 2, S):
                        hidden(s, q, 1)

                def vectors_if(q):
                    if 0 <= live(t, 2, S):
                        vectors(s, q)

                def pick_if(half):
                    if 0 <= live(t, 0, S):
                        pick_sum(t, r % 2, half)

                def add(first, last):
                    if live(t, 4, S) < 0:
                        return
                    s4, k4 = t - 4, (r - 4) % 2
                    add_sources(s4, k4, range(first, last), hots, prod2, prod2_made, hots2_made, None)
                    if first == 0 and not early(s4, 1):
                        pe.wait_ge(wtile_out, s4)
                    for c in range(first, last):
                        ins = T.matmul(mm[:, 1, 0:WIN * YW], win_hot[:, k4, c, :],
                                       win_prod[:, k4, c].rearrange("p w m -> p (w m)"), start=(c == 0),
                                       stop=False, skip_group_check=True)
                    if last == CH:
                        ins.then_inc(scattered2, 1)

                if isinstance(t, int) and t == S + 3:
                    pe.wait_ge(v_out, 2 * S)
                    keep_warm(42)
                rows_if(0)
                add(0, 2)
                hidden_if(0)
                rows_if(1)
                add(2, 4)
                vectors_if(0)
                hidden_if(1)
                rows_if(2)
                add(4, 6)
                vectors_if(1)
                hidden_if(2)
                rows_if(3)
                add(6, 8)
                vectors_if(2)
                hidden_if(3)
                add(8, 10)
                vectors_if(3)
                add(10, 12)
                pick_if(0)
                add(12, 14)
                pick_if(1)
                add(14, 16)

            def front(s, k):
                for q in range(Q):
                    turn(s, k, q)
                    if q >= 1:
                        messages(s, k, q - 1, 1)
                messages(s, k, Q - 1, 1)

            def back(s, k):
                pe.wait_ge(prod_made, s + 1)
                for c in range(CH):
                    pe.wait_ge(hot_made, s * CH + c + 1)
                    for b in range(NB):
                        ins = T.matmul(acc[:, b // 2, (b % 2) * GW:(b % 2) * GW + GW],
                                       hot[:, c % 4, b * P:(b + 1) * P],
                                       prod[:, k, c].rearrange("p a m -> p (a m)"),
                                       start=False, stop=False, skip_group_check=True)
                    for b in range(NB):
                        ins = T.matmul(acc[:, 2, GW + b * NA:GW + (b + 1) * NA],
                                       dhot[:, c % 4, b * P:(b + 1) * P],
                                       in_span[1][:, bass.ds(s * CH + c, 1), :, 0].rearrange("p o a -> p (o a)"),
                                       start=False, stop=False, skip_group_check=True)
                    ins.then_inc(hot_used, 1)

            def front2(s, k):
                def arrived():
                    pe.wait_ge(rows2_in[k], landed(s, k, 2 * CH))

                layer_rows(s, k, 0, 2, arrived)
                layer_rows(s, k, 1, 2, arrived)
                hidden(s, 0, 2)
                layer_rows(s, k, 2, 2, arrived)
                hidden(s, 1, 2)
                vectors(s, 0)
                layer_rows(s, k, 3, 2, arrived)
                hidden(s, 2, 2)
                vectors(s, 1)
                hidden(s, 3, 2)
                vectors(s, 2)
                vectors(s, 3)

            def back2(s, k):
                for w in range(2):
                    pe.wait_ge(prod2_made, 2 * s + w + 1)
                    for c in range(CH):
                        pe.wait_ge(hot2_made, (2 * s + w) * CH + c + 1)
                        for b in range(NB):
                            ins = T.matmul(acc[:, b // 2, (b % 2) * YG:(b % 2) * YG + YG],
                                           hot[:, c % 4, b * P:(b + 1) * P],
                                           prod2[:, w, c].rearrange("p a m -> p (a m)"),
                                           start=False, stop=False, skip_group_check=True)
                        ins.then_inc(hot2_used, 1)

            def turn_and_apply(source, weights, ready, first):
                pe.wait_ge(node_dve, ready)
                for g in range(4):
                    ins = T.transpose(tp[:, 0, g * P:(g + 1) * P],
                                      source[:, g * 8:(g + 1) * 8, :].rearrange("p g d -> p (g d)"), ident[:])
                ins.then_inc(node_pe, 1)
                pe.wait_ge(node_act, first)
                for g in range(4):
                    ins = T.matmul(mm[:, 0, g * P:(g + 1) * P], turned[:, 0, g * P:(g + 1) * P], weights[:],
                                   start=True, stop=True)
                ins.then_inc(node_pe, 1)

            def upd_turn(n):
                if 2 * n % UPD_PIECE == 0:
                    pe.wait_ge(node_dve, 3 + 2 * n // UPD_PIECE)
                if n >= 2:
                    pe.wait_ge(node_act, n)
                last = min(2, BLOCKS - 2 * n)
                for j in range(last * 2):
                    ins = T.transpose(tp[:, n % 2, j * P:(j + 1) * P],
                                      nouter[:, 2 * n + j // 2, (j % 2) * 8:(j % 2) * 8 + 8, :]
                                      .rearrange("p i h -> p (i h)"), ident[:])
                ins.then_inc(node_pe, 1)

            def upd_apply(n):
                pe.wait_ge(node_act, n + 2)
                for j in range(min(2, BLOCKS - 2 * n)):
                    blk = 2 * n + j
                    for half in range(2):
                        ins = T.matmul(mm[:, 1, blk * D:(blk + 1) * D],
                                       turned[:, n % 2, (2 * j + half) * P:(2 * j + half + 1) * P],
                                       w_upd[:, half, :], start=(half == 0), stop=(half == 1))
                ins.then_inc(node_pe, 1)

            def keep_warm(products):
                for _ in range(products):
                    T.matmul(vv[:, :], zeros[:, 0:P], zeros[:], start=True, stop=True)

            def node_update():
                keep_warm(6)
                turn_and_apply(agg, bd_msg, 1, 1)
                keep_warm(12)
                upd_turn(0)
                for n in range(1, UPD):
                    upd_turn(n)
                    upd_apply(n - 1)
                upd_apply(UPD - 1)
                keep_warm(5)
                turn_and_apply(aggl, bd_upd, 3 + -(-BLOCKS // UPD_PIECE), UPD + 3)
                pe.wait_ge(sums_out, 3)
                clear_acc(acc2_zero)

            def mark(done):
                T.matmul(vv[0:2, 0:2], zeros[:, 0:2], zeros[:, 0:2], start=True, stop=True).then_inc(done, 1)

            pe.wait_ge(consts_ready, 1)
            clear_acc(acc_zero)
            find_windows()
            pe.wait_ge(weights_in, 16 * N_WEIGHT_DMAS)
            pe.wait_ge(near_known, 1)
            is_near = pe.value_load(near_i[0:1, 0:1], min_val=0, max_val=1)
            with pe.If(is_near == 1):
                run_steps(pe, S, near_first, 4)
                mark(acc_done)
                pe.wait_ge(cnt_out, 1)
                T.transpose(tp[0:S * WIN, 1, 0:P], counts[:].rearrange("p s w -> p (s w)"), ident[:]).then_inc(cnt_pe, 1)
                pe.wait_ge(cnt_out, 2)
                T.matmul(tp[:, 1, 0:BLOCKS], counts_t[:], select[:], start=True, stop=True).then_inc(cnt_pe, 1)
                node_update()
                run_steps(pe, S, near_second, 4)
                mark(acc2_done)
            with pe.Else():
                find_bound()
                run_tiles(pe, S, front, back)
                mark(acc_done)
                node_update()
                run_tiles(pe, S, front2, back2)
                mark(acc2_done)

        @block.scalar
        def _(act):
            A = nc.scalar

            def copy_turned(s, q):
                act.wait_ge(turned_pe, s * Q + q + 1)
                if not (early(s, 1) and q < 2):
                    act.wait_ge(msg_pe, s * Q + q - 1)
                A.activation(outer_t[:, q % 2, 0:QC * EP], tp[:, q % 2, 0:QC * EP], ACT.Copy).then_inc(turned_out, 1)

            def out_messages(s, k, slot):
                act.wait_ge(msg_pe, s * Q + Q)
                if not early(s, 2):
                    act.wait_ge(part_made, s - 1)
                A.activation(msg[:, k].rearrange("p c t d -> p (c t d)")[:, 0:CH * D],
                             mm[0:EP, k * slot, 0:CH * D], ACT.Silu,
                             scale=float(KM) ** -0.5).then_inc(msg_made, 1)

            def place_window(s, k, target, table, width, picked_by, count, made):
                if not early(s, 2):
                    act.wait_ge(picked_by, count)
                first = act.value_load(base_i[0:1, bass.ds(s, 1)], min_val=0, max_val=BLOCKS - 1)
                A.activation(target[:, k, :, 0:width], table[:, bass.ds(first, WIN), 0:width],
                             ACT.Copy).then_inc(made, 1)

            def count(s, k, w):
                if w == 0:
                    act.wait_ge(hot_t_made, WIN * (s + 1))
                if not (early(s, 1) and w == 0):
                    act.wait_ge(counted, WIN * s + w)
                A.activation(count_junk, hot_t[:, k, w, 0:TE], ACT.Copy,
                             accum_out=counts[:, bass.ds(s, 1), w]).then_inc(counted, 1)

            def near_first(t, r):
                def next_window(s, k):
                    place_window(s, k, win_tab, rows_tab, XW, picked_pe, 2 * (s - 1), win_tab_made)

                if isinstance(t, int) and t == 0:
                    next_window(0, 0)
                for q in range(Q):
                    if 0 <= live(t, 2, S):
                        copy_turned(t - 2, q)
                    if 0 <= live(t, 0, S) and q in (1, 2):
                        half = q - 1
                        act.wait_ge(picked_pe, 2 * t + half + 1)
                        if half == 0 and not early(t, 1):
                            act.wait_ge(xj_made, t)
                        A.activation(picked[:, half * HALF * XW:(half + 1) * HALF * XW],
                                     (mm[0:EP, 1, :], vv[0:EP, :])[half][:, 0:HALF * XW],
                                     ACT.Copy).then_inc(picked_out, 1)
                        if half == 1:
                            count(t, r % 2, 0)
                if not isinstance(t, int) or t + 1 < S:
                    next_window(t + 1, (r + 1) % 2)
                if 0 <= live(t, 2, S):
                    out_messages(t - 2, (r - 2) % 2, 0)
                if 0 <= live(t, 0, S):
                    count(t, r % 2, 1)

            def copy_rows(s, q, banks):
                act.wait_ge(xt_pe, s * Q + q + 1)
                if not (early(s, 1) and q < 2):
                    act.wait_ge(h_pe, s * Q + q - 1)
                A.activation(x_t[:, q % 2, :], tp[:, q % banks, 0:2 * EP], ACT.Copy).then_inc(xt_out, 1)

            def relu(s, q, banks):
                act.wait_ge(h_pe, s * Q + q + 1)
                if not (early(s, 1) and q < 2):
                    act.wait_ge(v_pe, s * Q + q - 1)
                A.activation(h[:, q % 2, 0:QC * EP], mm[:, q % banks, 0:QC * EP], ACT.Relu,
                             bias=bias1[:, 0:1], scale=1.0 / Z_SCALE).then_inc(h_out, 1)

            def copy_vectors(s, k):
                act.wait_ge(v_pe, (s + 1) * Q)
                if not early(s, 2):
                    act.wait_ge(msg2_made, s - 1)
                A.activation(v[:, k].rearrange("p c t d -> p (c t d)"), vv[0:EP, :], ACT.Copy).then_inc(v_out, 1)
                A.activation(vsq[:, k].rearrange("p c t d -> p (c t d)"), vv[0:EP, :], ACT.Square).then_inc(v_out, 1)

            def turned_onehots(s, k, q):
                cols = slice(q * QC * EP, (q + 1) * QC * EP)
                act.wait_ge(dst2_in[k], landed(s, k, 1))
                if not (early(s, 1) and q == 0):
                    act.wait_ge(hot_t_act, s * Q + q)
                act.sem_inc(act_held, 1)
                A.activation(distance[:], dst_all[:, k, cols], ACT.Abs,
                             bias=minus_node[:, bass.ds(s, 1)]).then_inc(distances, 1)
                act.wait_ge(distances, s * Q + q + 1)
                A.activation(hot_t2[:, k, WIN - 1, cols], distance[:], ACT.Relu, bias=ones_col[:, 0:1],
                             scale=-1.0).then_inc(hot_t_act, 1)

            def near_second(t, r):
                def next_window(s, k):
                    place_window(s, k, win_tab2, rows_tab2, PARTS2 * RW, picked2_pe, s - 1, win_tab2_made)

                if isinstance(t, int) and t == 0:
                    next_window(0, 0)
                for q in range(Q):
                    if 0 <= live(t, 2, S):
                        copy_rows(t - 2, q, 1)
                    if 0 <= live(t, 0, S):
                        turned_onehots(t, r % 2, q)
                    if 0 <= live(t, 2, S):
                        relu(t - 2, q, 1)
                if 0 <= live(t, 2, S):
                    copy_vectors(t - 2, (r - 2) % 2)
                if not isinstance(t, int) or t + 1 < S:
                    next_window(t + 1, (r + 1) % 2)
                if 0 <= live(t, 0, S):
                    act.wait_ge(picked2_pe, t + 1)
                    if not early(t, 4):
                        act.wait_ge(rows_read, t - 3)
                    A.activation(gath[:, r % 4, :, 2:4, :], tp[0:EP, 1, 0:CH * RW].rearrange("p (c f d) -> p c f d", c=CH, f=2),
                                 ACT.Copy).then_inc(picked2_out, 1)
                if 0 <= live(t, 4, S):
                    act.wait_ge(scattered2, t - 4 + 1)
                    if not early(t - 4, 1):
                        act.wait_ge(wsum_added, t - 4)
                    A.activation(wtile[:], mm[:, 1, 0:WIN * YW], ACT.Copy, scale=1.0 / Z_SCALE).then_inc(wtile_out, 1)

            def front2(s, k):
                copy_rows(s, 0, 2)
                copy_rows(s, 1, 2)
                relu(s, 0, 2)
                copy_rows(s, 2, 2)
                relu(s, 1, 2)
                copy_rows(s, 3, 2)
                relu(s, 2, 2)
                relu(s, 3, 2)
                copy_vectors(s, k)

            def out_messages_two(s, k):
                for q in range(Q):
                    copy_turned(s, q)
                out_messages(s, k, 1)

            def none(s, k):
                pass

            def copy_sums(done, out_sem, scale=1.0):
                act.wait_ge(done, 1)
                for bank in range(3):
                    A.activation(sums[:, bank, :], acc[:, bank, :], ACT.Copy, scale=scale).then_inc(out_sem, 1)

            def give_root(value):
                A.activation(root[:], value[:], ACT.Sqrt).then_inc(root_given, 1)

            def node_update():
                act.wait_ge(node_pe, 1)
                A.activation(turned[:, 0, :], tp[:, 0, :], ACT.Copy).then_inc(node_act, 1)
                act.wait_ge(node_dve, 2)
                give_root(deg)
                for n in range(UPD):
                    act.wait_ge(node_pe, 3 + (0 if n == 0 else 2 * n - 1))
                    if n >= 2:
                        act.wait_ge(node_pe, 3 + 2 * (n - 1))
                    w = min(4, 2 * (BLOCKS - 2 * n)) * P
                    A.activation(turned[:, n % 2, 0:w], tp[:, n % 2, 0:w], ACT.Copy).then_inc(node_act, 1)
                act.wait_ge(node_pe, 2 + 2 * UPD)
                A.activation(aggl[:, 0:BLOCKS, :].rearrange("p b d -> p (b d)"), mm[:, 1, 0:BLOCKS * D], ACT.Silu,
                             scale=float(D * D) ** -0.5).then_inc(node_act, 1)
                act.wait_ge(node_pe, 3 + 2 * UPD)
                A.activation(turned[:, 0, :], tp[:, 0, :], ACT.Copy).then_inc(node_act, 1)
                act.wait_ge(root_asked, 1)
                give_root(stat)

            act.wait_ge(attr_all_in, 16)
            A.activation(attr_all, attr_all, ACT.Abs).then_inc(attr_abs, 1)
            act.wait_ge(near_known, 1)
            is_near = act.value_load(near_i[0:1, 0:1], min_val=0, max_val=1)
            with act.If(is_near == 1):
                act.wait_ge(tab_made, 1)
                run_steps(act, S, near_first, 2)
                copy_sums(acc_done, sums_out)
                act.wait_ge(cnt_pe, 1)
                A.activation(counts_t[:], tp[0:S * WIN, 1, 0:P], ACT.Copy).then_inc(cnt_out, 1)
                node_update()
                act.wait_ge(tab_made, 2)
                run_steps(act, S, near_second, 4)
                copy_sums(acc2_done, sums2_out, 1.0 / Z_SCALE)
            with act.Else():
                run_tiles(act, S, out_messages_two, none)
                copy_sums(acc_done, sums_out)
                node_update()
                run_tiles(act, S, front2, none)
                copy_sums(acc2_done, sums2_out, 1.0 / Z_SCALE)
            act.wait_ge(root_asked, 2)
            give_root(stat)

        @block.vector
        def _(dve):
            V = nc.vector
            ch = Chain(dve, setup)
            link = ch.link
            V.memset(zeros[:], 0.0)
            V.memset(xn[:], 0.0)
            V.memset(agg[:], 0.0)
            V.memset(aggl[:], 0.0)
            V.memset(bd_msg[:], 0.0)
            V.memset(bd_upd[:], 0.0)
            V.memset(w1[:], 0.0)
            V.memset(w2[:], 0.0)
            V.memset(ones_row[:], 1.0)
            V.memset(ones_parts[:], 1.0)
            V.memset(ones_col[:], 1.0)
            V.memset(maxima[:], 0.0)
            V.memset(minima[:], 0.0)
            V.memset(base_i[:, S:S + 1], 0)
            V.memset(idx[0][:, C:C + CH], 0)
            V.memset(rows_tab[:], 0.0)
            link(V.memset(parts, 1.0))
            dve.wait_ge(iota_made, 4)
            link(V.tensor_copy(part_id[:], iota_p[:]))
            link(V.tensor_scalar(ident[:], iota_n[:, 0:P], part_id[:, 0:1], None, ALU.is_equal))
            V.tensor_scalar(part_id[:], part_id[:], 1.0, None, ALU.mult).then_inc(consts_ready, 1)
            dve.wait_ge(consts_ready, 1)
            dve.wait_ge(idx_in, 48)
            V.tensor_copy(dst_short[:], dst_int).then_inc(dst16_made, 1)

            def place(which):
                link(V.tensor_copy(fidx, idx[which][:, 0:C]))
                link(V.tensor_scalar(span, fidx, float(NT), None, ALU.is_ge))
                for a in range(2, NA):
                    link(V.scalar_tensor_tensor(out=span, in0=fidx, scalar=float(NT * a), in1=span,
                                                op0=ALU.is_ge, op1=ALU.add))
                link(V.scalar_tensor_tensor(out=within[which][:], in0=span, scalar=-float(NT), in1=fidx,
                                            op0=ALU.mult, op1=ALU.add))
                for twice in range(2):
                    ins = V.tensor_copy(span_twice[:, :, twice], span)
                link(ins)
                link(V.tensor_tensor(in_span[which], bcast(iota_twice[0:EP].unsqueeze(1), (EP, C, NA, 2)),
                                     bcast(span_twice.unsqueeze(2), (EP, C, NA, 2)), ALU.is_equal))

            link(V.tensor_copy(fidx, idx[1][:]))
            tiles_of = fidx.rearrange("p (s c) -> p s c", c=CH)
            link(V.tensor_reduce(ends[:, 0, :], tiles_of, AX, ALU.min))
            link(V.tensor_reduce(ends[:, 1, :], tiles_of, AX, ALU.max))
            V.tensor_scalar(ends[:, 1, :], ends[:, 1, :], -1.0, None, ALU.mult).then_inc(ends_dve, 1)
            dve.wait_ge(ends_pe, 1)
            V.tensor_reduce(end_col[:], tp[0:2 * S, 0, 0:EP], AX, ALU.min).then_inc(ends_dve, 1)
            dve.wait_ge(ends_pe, 2)
            link(V.tensor_copy(end_row[:].rearrange("p t s -> p (t s)"), tp[0:1, 1, 0:2 * S]))
            link(V.tensor_tensor(passed, bcast(end_row[:, 0, :].unsqueeze(2), (1, S, BLOCKS - 1)),
                                 bcast(block_start[:].unsqueeze(1), (1, S, BLOCKS - 1)), ALU.is_ge))
            link(V.tensor_reduce(base[:], passed, AX, ALU.add))
            link(V.tensor_copy(base_i[:, 0:S], base[:]))
            link(V.scalar_tensor_tensor(out=near_row[:], in0=base[:], scalar=float(P), in1=end_row[:, 1, :],
                                        op0=ALU.mult, op1=ALU.add))
            link(V.tensor_scalar(near_row[:], near_row[:], -float(WIN * P), None, ALU.is_gt))
            link(V.tensor_reduce(near[:], near_row[:], AX, ALU.min))
            for w in range(WIN):
                ins = V.tensor_scalar(base_row[:, :, w], base[:], float(w), None, ALU.add)
            ins.then_inc(ends_dve, 1)
            dve.wait_ge(ends_dve, 3)
            V.tensor_copy(near_i[:], near[:]).then_inc(near_known, 1)
            dve.wait_ge(ends_pe, 3)
            link(V.tensor_scalar(window[:].rearrange("p s w -> p (s w)"), mm[:, 0, 0:S * WIN], float(P), None,
                                 ALU.mult))
            for twice in range(2):
                ins = V.tensor_tensor(within_win[:, :, twice].rearrange("p (s c) -> p s c", c=CH), tiles_of,
                                      bcast(window[0:EP, :, 0].unsqueeze(2), (EP, S, CH)), ALU.subtract)
            link(ins)
            link(V.tensor_scalar(window[:].rearrange("p s w -> p (s w)"), window[:].rearrange("p s w -> p (s w)"),
                                 part_id[:, 0:1], None, ALU.add))
            link(V.tensor_scalar(minus_node[:], window[:, :, WIN - 1], -1.0, None, ALU.mult))
            link(V.tensor_copy(base_col[:], mm[0:S * WIN, 1, 0:1]))
            link(V.tensor_scalar(select[:], iota_n[0:S * WIN, 0:BLOCKS], base_col[:, 0:1], None, ALU.is_equal))

            schain = Chain(dve, split_chain, 1)
            wchain = Chain(dve, split2_chain, 2)
            nch = Chain(dve, node_chain)
            nl = nch.link

            def find_scale():
                dve.wait_ge(attr_abs, 1)
                dve.wait_ge(weights_in, 16 * N_WEIGHT_DMAS)
                V.tensor_reduce(maxima[0:EP, 0:1], attr_all, AX, ALU.max)
                for i, values in enumerate((xn[:].rearrange("p b d -> p (b d)"), w_msg[:])):
                    V.tensor_reduce(maxima[:, i + 1:i + 2], values, AX, ALU.max)
                    ins = V.tensor_reduce(minima[:, i + 1:i + 2], values, AX, ALU.min)
                link(ins)
                V.scalar_tensor_tensor(out=maxima[:], in0=minima[:], scalar=-1.0, in1=maxima[:], op0=ALU.mult,
                                       op1=ALU.max).then_inc(bound_dve, 1)
                dve.wait_ge(bound_pe, 1)
                V.tensor_reduce(max_col[:], mm[0:3, 0, CH * D:CH * D + P], AX, ALU.max).then_inc(bound_dve, 1)
                dve.wait_ge(bound_pe, 2)
                link(V.tensor_copy(bound[:, 0:3], mm[0:1, 0, CH * D + P:CH * D + P + 3]))
                link(V.tensor_tensor(bound[:, 3:4], bound[:, 0:1], bound[:, 1:2], ALU.mult))
                link(V.scalar_tensor_tensor(out=bound[:, 3:4], in0=bound[:, 3:4], scalar=float(KM) ** 0.5,
                                            in1=bound[:, 2:3], op0=ALU.mult, op1=ALU.mult))
                link(V.tensor_scalar(bound[:, 3:4], bound[:, 3:4], 2.0 ** -100, 2.0 ** 100, ALU.max, ALU.min))
                bits, exponent = power[:].bitcast(I32), 0x7F800000
                link(V.tensor_scalar(bits[:, 0:1], bound[:, 3:4].bitcast(I32), exponent, None, ALU.bitwise_and))
                link(V.tensor_scalar(bits[:, 1:2], bits[:, 0:1], exponent, None, ALU.bitwise_xor))
                V.tensor_scalar(scale_row[:, 0:1], power[:, 1:2], 2.0 ** 13, None, ALU.mult)
                V.tensor_scalar(scale_row[:, 1:2], power[:, 0:1], 2.0 ** -14, None, ALU.mult).then_inc(bound_dve, 1)
                dve.wait_ge(bound_pe, 3)
                V.tensor_copy(scale[:], mm[:, 0, CH * D + P + 4:CH * D + P + 6]).then_inc(bound_dve, 1)
                dve.wait_ge(bound_dve, 4)

            def split_messages(s, k, more=None):
                schain.step(s)
                dve.wait_ge(msg_made, s + 1)
                m = msg[:, k].rearrange("p c t d -> p (c t d)")[:, 0:CH * D].rearrange("p (c d) -> p c d", c=CH)
                if not early(s, 1):
                    dve.wait_ge(prod_made, s)
                schain.link(V.tensor_scalar(parts[:, :, 0:D], m, scale[0:EP, 0:1], None, ALU.mult), more)
                V.scalar_tensor_tensor(out=parts[:, :, D:2 * D], in0=m, scalar=scale[0:EP, 0:1],
                                       in1=parts[:, :, 0:D], op0=ALU.mult, op1=ALU.subtract).then_inc(part_made, 1)
                if more is not None:
                    more()
                dve.wait_ge(part_made, s + 1)

            def spread(target, which, s, source, width):
                place_of = in_block if which is None else in_span[which]
                full = (EP, CH, place_of.shape[2], width // 2, 2)
                return V.tensor_tensor(
                    target.rearrange("p c a (m t) -> p c a m t", t=2),
                    bcast(source.rearrange("p c (m t) -> p c m t", t=2).unsqueeze(2), full),
                    bcast(place_of[:, bass.ds(s * CH, CH), :, :].unsqueeze(3), full), ALU.mult)

            def make_outer(s, k):
                if not early(s, 2):
                    dve.wait_ge(turned_pe, (s - 1) * Q)
                V.tensor_tensor(outer[:, k], bcast(xj[:, k].unsqueeze(3), (EP, CH, D, DE)),
                                bcast(attr[:, k].unsqueeze(2), (EP, CH, D, DE)), ALU.mult).then_inc(outer_made, 1)

            def turned_onehots(s, k, arrived, picked, count, made):
                dve.wait_ge(arrived[k], landed(s, k, 1))
                if not early(s, 2):
                    dve.wait_ge(picked, count)
                    if made is hot_t_made:
                        dve.wait_ge(counted, WIN * (s - 1))
                first_layer = made is hot_t_made
                for w in range(WIN if first_layer else WIN - 1):
                    V.tensor_scalar((hot_t if first_layer else hot_t2)[:, k, w, 0:TE], dst_all[:, k, :], window[:, bass.ds(s, 1), w], None,
                                    ALU.is_equal).then_inc(made, 1)

            class onehots_between:

                def __init__(self, s, k, onehot):
                    self.s, self.k, self.onehot, self.c = s, k, onehot, 0

                def __call__(self):
                    if self.c < CH - 1:
                        self.emit()

                def emit(self):
                    self.c += 1
                    return V.tensor_scalar(self.onehot[:, self.k, self.c - 1, :], iota_n[0:EP, :],
                                           within[0][:, bass.ds(self.s * CH + self.c - 1, 1)], None, ALU.is_equal)

                def rest(self, made):
                    while self.c < CH:
                        ins = self.emit()
                    ins.then_inc(made, 1)

            xchain = Chain(dve, xj_chain, 1)

            def near_first(t, r):
                if 0 <= live(t, 0, S):
                    turned_onehots(t, r % 2, dst_in, picked_pe, 2 * (t - 1), hot_t_made)
                if 0 <= live(t, 1, S):
                    s, k = t - 1, (r - 1) % 2
                    xchain.step(s)
                    dve.wait_ge(attr_in[k], landed(s, k, 1))
                    dve.wait_ge(picked_out, 2 * (s + 1))
                    rows = picked.rearrange("p (c t d) -> p c t d", c=CH, t=PARTS)
                    if not early(s, 2):
                        dve.wait_ge(outer_made, s - 1)
                    xchain.link(V.tensor_tensor(xj[:, k], rows[:, :, 0, :], rows[:, :, 1, :], ALU.add))
                    V.tensor_tensor(xj[:, k], xj[:, k], rows[:, :, 2, :], ALU.add).then_inc(xj_made, 1)
                    dve.wait_ge(xj_made, s + 1)
                    make_outer(s, k)
                if isinstance(t, int) and t == 2:
                    find_scale()
                if 0 <= live(t, 3, S):
                    s, k = t - 3, (r - 3) % 2
                    if not early(s, 2):
                        dve.wait_ge(scattered, s - 1)
                    more = onehots_between(s, k, hots)
                    split_messages(s, k, more)
                    spread(prod[:, k], 0, s, parts, MW).then_inc(prod_made, 1)
                    more.rest(hots_made)

            full = (EP, CH, 2, D)
            hchain = Chain(dve, house_chain, 11)

            def reflect(s, k, slot, more):
                hchain.step(s)

                def lk(ins):
                    hchain.link(ins, more)

                z = gath[:, slot][:, :, 0:4:3, :]
                m = msg[:, k]
                vk = v[:, k]
                lk(V.tensor_reduce(rnorm[:], vsq[:, k], AX, ALU.add))
                lk(V.tensor_scalar(rnorm[:], rnorm[:], UNIT_FLOOR ** 2, 0.5, ALU.max, ALU.mult))
                lk(V.reciprocal(rnorm[:], rnorm[:]))
                lk(V.tensor_tensor(sq, vk, z, ALU.mult))
                lk(V.tensor_reduce(scal[:], sq, AX, ALU.add))
                lk(V.tensor_tensor(scal[:], scal[:], rnorm[:], ALU.mult))
                lk(V.tensor_tensor(sq, vk, bcast(scal[:].unsqueeze(3), full), ALU.mult))
                V.tensor_tensor(t1, z, sq, ALU.subtract).then_inc(rows_read, 1)
                if more is not None:
                    more()
                dve.wait_ge(rows_read, s + 1)
                if more is not None and not (isinstance(s, int) and s + 4 >= S):
                    V.tensor_copy(idx_now[:, slot, 0, :], idx[0][:, bass.ds((s + 4) * CH, CH)]).then_inc(sources_placed, 1)
                for w in range(2):
                    ins = V.tensor_tensor(sq[:, :, w, :], vk[:, :, w, :], t1[:, :, 1 - w, :], ALU.mult)
                lk(ins)
                lk(V.tensor_reduce(scal[:], sq, AX, ALU.add))
                lk(V.tensor_tensor(scal[:], scal[:], rnorm[:], ALU.mult))
                lk(V.tensor_tensor(sq, vk, bcast(scal[:].unsqueeze(3), full), ALU.mult))
                for w in range(2):
                    ins = V.tensor_tensor(m[:, :, w, :], t1[:, :, 1 - w, :], sq[:, :, w, :], ALU.subtract)
                ins.then_inc(msg2_made, 1)
                if more is not None:
                    more()
                dve.wait_ge(msg2_made, s + 1)

            def split_both(s, k, more):
                wchain.step(s)

                def lk(ins):
                    wchain.link(ins, more)

                m = msg[:, k]

                def part(i):
                    return parts2[:, k, :, :, i * D:(i + 1) * D].rearrange("p w c d -> p c w d")

                lk(V.tensor_copy(part(0), m))
                lk(V.tensor_tensor(part(1), m, part(0), ALU.subtract))

            def add_window(s):
                dve.wait_ge(wtile_out, s + 1)
                first = dve.value_load(base_i[0:1, bass.ds(s, 1)], min_val=0, max_val=BLOCKS - 1)
                there = wsum[:, bass.ds(first, WIN), :]
                V.tensor_tensor(there, there, wtile[:].rearrange("p (w m) -> p w m", w=WIN),
                                    ALU.add).then_inc(wsum_added, 1)

            def near_second(t, r):
                if 0 <= live(t, 0, S):
                    turned_onehots(t, r % 2, dst2_in, picked2_pe, t - 1, hot_t2_made)
                if 0 <= live(t, 3, S):
                    s, k, slot = t - 3, (r - 3) % 2, (r - 3) % 4
                    if not early(s, 2):
                        dve.wait_ge(scattered2, s - 1)
                    dve.wait_ge(near_rows[slot], landed(s, slot, CH, 4))
                    dve.wait_ge(picked2_out, s + 1)
                    dve.wait_ge(v_out, 2 * (s + 1))
                    more = onehots_between(s, k, hots)
                    reflect(s, k, slot, more)
                if 0 <= live(t, 5, S):
                    add_window(t - 5)
                if 0 <= live(t, 3, S):
                    V.tensor_tensor(win_hot[:, k].rearrange("p c (n t) -> p c n t", t=2),
                                    bcast(iota_n[0:EP, 0:P].rearrange("p (n t) -> p n t", t=2).unsqueeze(1),
                                          (EP, CH, P // 2, 2)),
                                    bcast(within_win[:, bass.ds(s * CH, CH), :].unsqueeze(2), (EP, CH, P // 2, 2)),
                                    ALU.is_equal)
                    split_both(s, k, more)
                    spread(win_prod[:, k], None, s, parts2[:, k, 1], YW)
                    spread(prod2[:, k], 0, s, parts2[:, k, 0], YW).then_inc(prod2_made, 1)
                    more.rest(hots2_made)

            def front(s, k):
                dve.wait_ge(attr_in[k], landed(s, k, 1))
                dve.wait_ge(rows_in[k], landed(s, k, CH))
                make_outer(s, k)

            def back(s, k):
                split_messages(s, k)
                if not early(s, 2):
                    dve.wait_ge(hot_used, (s - 1) * CH)
                spread(prod[:, k], 0, s, parts, MW).then_inc(prod_made, 1)
                for c in range(CH):
                    if not (early(s, 1) and c < 4):
                        dve.wait_ge(hot_used, s * CH + c - 3)
                    V.tensor_scalar(dhot[:, c % 4, :], iota_n[0:EP, :], within[1][:, bass.ds(s * CH + c, 1)], None,
                                    ALU.is_equal)
                    V.tensor_scalar(hot[:, c % 4, :], iota_n[0:EP, :], within[0][:, bass.ds(s * CH + c, 1)], None,
                                    ALU.is_equal).then_inc(hot_made, 1)

            def nothing(s, k):
                pass

            def back2(s, k):
                dve.wait_ge(v_out, 2 * (s + 1))
                dve.wait_ge(rows2_in[k], landed(s, k, 2 * CH))
                reflect(s, k, k, None)
                split_both(s, k, None)
                for w in range(2):
                    if not early(s, 1):
                        dve.wait_ge(hot2_used, (2 * s + w - 1) * CH)
                    spread(prod2[:, w], w, s, parts2[:, k, w], YW).then_inc(prod2_made, 1)
                    for c in range(CH):
                        if not (early(s, 1) and w == 0 and c < 4):
                            dve.wait_ge(hot2_used, (2 * s + w) * CH + c - 3)
                        V.tensor_scalar(hot[:, c % 4, :], iota_n[0:EP, :], within[w][:, bass.ds(s * CH + c, 1)], None,
                                        ALU.is_equal).then_inc(hot2_made, 1)

            def sum_parts(target, width, parts_in, done=None):
                for i in range(1, parts_in):
                    for b in range(NB):
                        cols = sums[:, b // 2, (b % 2) * NA * width:(b % 2 + 1) * NA * width].rearrange(
                            "p (a m) -> p a m", a=NA)
                        at = target[:, b:BLOCKS:NB, :]
                        ins = V.tensor_tensor(at, cols[:, :, 0:D] if i == 1 else at, cols[:, :, i * D:(i + 1) * D],
                                              ALU.add)
                    if i == parts_in - 1 and done is not None:
                        ins.then_inc(done, 1)
                    else:
                        nl(ins)

            def inverse_root(value, target, turn):
                dve.wait_ge(root_given, turn)
                nl(V.reciprocal(target, root[:]))
                nl(V.tensor_tensor(newton[:], target, target, ALU.mult))
                nl(V.tensor_tensor(newton[:], newton[:], value, ALU.mult))
                nl(V.tensor_scalar(newton[:], newton[:], -0.5, 1.5, ALU.mult, ALU.add))
                nl(V.tensor_tensor(target, target, newton[:], ALU.mult))

            b3 = (P, BLOCKS, D)

            def layernorm(values, scratch, target, turn):
                nl(V.tensor_reduce(stat[:], values[:], AX, ALU.add))
                nl(V.tensor_scalar(stat[:], stat[:], 1.0 / D, None, ALU.mult))
                nl(V.tensor_tensor(values[:], values[:], bcast(stat[:].unsqueeze(2), b3), ALU.subtract))
                nl(V.tensor_tensor(scratch[:], values[:], values[:], ALU.mult))
                nl(V.tensor_reduce(stat[:], scratch[:], AX, ALU.add))
                V.tensor_scalar(stat[:], stat[:], 1.0 / D, NORM_EPS, ALU.mult, ALU.add).then_inc(root_asked, 1)
                dve.wait_ge(root_asked, turn - 1)
                inverse_root(stat[:], inv[:], turn)
                nl(V.tensor_tensor(target, values[:], bcast(inv[:].unsqueeze(2), b3), ALU.mult))

            def make_table():
                tab = rows_tab2.rearrange("p b (t r) -> p b t r", t=PARTS2)[:, 0:BLOCKS]
                columns = ((xz[:, :, D:2 * D], 0), (xz[:, :, 0:D], D))
                for source, col in columns:
                    ins = V.tensor_copy(tab[:, :, 0, col:col + D], source)
                nl(ins)
                for source, col in columns:
                    ins = V.tensor_tensor(tab[:, :, 1, col:col + D], source, tab[:, :, 0, col:col + D], ALU.subtract)
                ins.then_inc(tab_made, 1)

            def split_bias():
                dve.wait_ge(weights_in, 16 * N_WEIGHT_DMAS)
                for i in range(1, PARTS):
                    nl(V.tensor_copy(bias2_parts[:], bias2[:]))
                    nl(V.tensor_scalar(past_row[:], part_id[0:PARTS, :], float(i), -1.0, ALU.is_ge, ALU.mult))
                    nl(V.scalar_tensor_tensor(out=bias2[:], in0=bias2_parts[:], scalar=past_row[:, 0:1], in1=bias2[:],
                                              op0=ALU.mult, op1=ALU.add))
                nl(V.tensor_copy(bias2_parts[:], bias2[:]))

            def node_update(in_degree):
                dve.wait_ge(sums_out, 3)
                sum_parts(agg, MW, PARTS2, node_dve)
                for b in range(NB):
                    cols = sums[:, b // 2, (b % 2) * GW:(b % 2 + 1) * GW].rearrange("p (a m) -> p a m", a=NA)
                    ins = V.tensor_tensor(deg[:, b:BLOCKS:NB].unsqueeze(2), cols[:, :, PARTS2 * D:PARTS2 * D + 1],
                                          in_degree(b), ALU.add)
                nl(ins)
                V.tensor_scalar(deg[:], deg[:], DEG_FLOOR, None, ALU.max).then_inc(node_dve, 1)
                dve.wait_ge(node_dve, 2)
                dve.wait_ge(node_pe, 2)
                nl(V.tensor_scalar(aggl[:].rearrange("p b d -> p (b d)"), mm[:, 0, :], float(D) ** -0.5,
                                   scale[:, 1:2], ALU.mult, ALU.mult))
                for first in range(0, BLOCKS, UPD_PIECE):
                    b = slice(first, min(first + UPD_PIECE, BLOCKS))
                    full = (P, b.stop - first, D, D)
                    V.tensor_tensor(nouter[:, b], bcast(xn[:, b].unsqueeze(3), full),
                                    bcast(aggl[:, b, :].unsqueeze(2), full), ALU.mult).then_inc(node_dve, 1)
                inverse_root(deg[:], dis[:], 1)
                dve.wait_ge(node_act, 2 + UPD)
                V.tensor_copy(stat[:], deg[:]).then_inc(node_dve, 1)
                dve.wait_ge(node_pe, 4 + 2 * UPD)
                nl(V.tensor_scalar(tmp[:].rearrange("p b d -> p (b d)"), mm[:, 0, 0:BLOCKS * D], float(D) ** -0.5,
                                   None, ALU.mult))
                nl(V.scalar_tensor_tensor(out=tmp[:], in0=xn[:], scalar=2.0, in1=tmp[:], op0=ALU.mult, op1=ALU.add))
                layernorm(tmp, tmp2, x1[:], 2)
                V.tensor_scalar(newton[:], dis[:], 1.0, None, ALU.min)
                nl(V.tensor_scalar(xz[:, :, D:2 * D], x1[:], Z_SCALE, None, ALU.mult))
                V.tensor_tensor(xz[:, :, 0:D], xz[:, :, D:2 * D], bcast(newton[:].unsqueeze(2), b3),
                                ALU.mult).then_inc(table_ready, 1)
                dve.wait_ge(table_ready, 1)
                V.tensor_copy(xz[:, :, 2 * D:3 * D], xz[:, :, 0:D]).then_inc(table_ready, 1)

            def finish(extra):
                if extra:
                    dve.wait_ge(wsum_added, S)
                    V.tensor_tensor(tmp[:], wsum[:, 0:BLOCKS, 0:D], wsum[:, 0:BLOCKS, D:2 * D], ALU.add)
                dve.wait_ge(sums2_out, 3)
                sum_parts(tmp2, YW, PARTS2)
                if extra:
                    nl(V.tensor_tensor(tmp2[:], tmp2[:], tmp[:], ALU.add))
                nl(V.tensor_tensor(tmp2[:], tmp2[:], bcast(dis[:].unsqueeze(2), b3), ALU.mult))
                nl(V.tensor_tensor(tmp2[:], tmp2[:], x1[:], ALU.add))
                nl(V.tensor_scalar(tmp2[:], tmp2[:], 0.0, None, ALU.max))
                nl(V.tensor_tensor(tmp[:], tmp2[:], x1[:], ALU.add))
                layernorm(tmp, tmp2, tmp[:], 3)
                V.tensor_copy(stat[:], deg[:]).then_inc(out_ready, 1)

            is_near = dve.value_load(near_i[0:1, 0:1], min_val=0, max_val=1)
            chained = ch.k
            dve.wait_ge(nodes_in, 32)
            with dve.If(is_near == 1):
                V.memset(hot_t[:, :, :, TE:TEP], 0.0)
                tab = rows_tab[:, 0:BLOCKS]
                nl(V.tensor_copy(tab[:, :, 0:D], xn[:]))
                nl(V.tensor_tensor(tmp2[:], xn[:], tab[:, :, 0:D], ALU.subtract))
                nl(V.tensor_copy(tab[:, :, D:2 * D], tmp2[:]))
                V.tensor_tensor(tab[:, :, 2 * D:3 * D], tmp2[:], tab[:, :, D:2 * D], ALU.subtract).then_inc(tab_made, 1)
                place(0)
                run_steps(dve, S, near_first, 3)
                V.tensor_copy(idx_now[:, :, 0, :],
                              idx[0][:, 0:4 * CH].rearrange("p (k c) -> p k c", k=4)).then_inc(sources_placed, 1)
                split_bias()
                dve.wait_ge(counted, WIN * S)
                V.tensor_scalar(in_block[:, :, 0, :], within_win, float(P), None, ALU.is_lt)
                nl(V.tensor_scalar(in_block[:, :, 1, :], within_win, float(P), None, ALU.is_ge))
                nl(V.scalar_tensor_tensor(out=within_win, in0=in_block[:, :, 1, :], scalar=-float(P), in1=within_win,
                                          op0=ALU.mult, op1=ALU.add))
                dve.wait_ge(counted, WIN * S)
                V.memset(wsum[:], 0.0).then_inc(cnt_out, 1)
                dve.wait_ge(cnt_out, 2)
                dve.wait_ge(cnt_pe, 2)
                node_update(lambda b: tp[:, 1, b:BLOCKS:NB].unsqueeze(2))
                make_table()
                run_steps(dve, S, near_second, 5)
                finish(True)
            with dve.Else():
                nch.k, ch.k = 0, chained
                find_scale()
                place(0)
                place(1)
                run_tiles(dve, S, front, back)
                split_bias()
                node_update(lambda b: sums[:, 2, GW + b * NA:GW + (b + 1) * NA].unsqueeze(2))
                run_tiles(dve, S, nothing, back2)
                finish(False)


_INS = [("x", "x"), ("src", "src"), ("dst", "dst"), ("dst", "dst_flat"), ("edge_attr_8", "edge_attr"),
        ("L0_gnn_W_msg_tp", "w_msg_tp"), ("L0_gnn_W_msg_lin", "w_msg_lin"),
        ("L0_gnn_W_upd_tp", "w_upd_tp"), ("L0_gnn_W_upd_lin", "w_upd_lin"),
        ("L1_gnn_W1", "w1_t"), ("L1_gnn_b1", "b1"), ("L1_gnn_W2", "w2_t"), ("L1_gnn_b2", "b2")]


def kernel(**inputs):
    import numpy as np
    import concourse.bacc as bacc
    from concourse.bass_utils import run_bass_kernel_spmd

    nc = bacc.Bacc("TRN2", target_bir_lowering=False, num_devices=1)
    arrays, args = {}, []
    for given, name in _INS:
        a = np.asarray(inputs[given])
        if name in ("w1_t", "w2_t"):
            a = a.T
        elif name in ("src", "dst"):
            a = a.reshape(-1, EP).T
        elif name == "edge_attr":
            a = a.reshape(-1, CH, EP, a.shape[1]).transpose(0, 2, 1, 3).reshape(-1, EP, CH * a.shape[1])
        a = np.ascontiguousarray(a)
        arrays[name] = a
        args.append(nc.dram_tensor(name, a.shape, mybir.dt.from_np(a.dtype), kind="ExternalInput").ap())
    shape = inputs["x"].shape
    args.append(nc.dram_tensor("out", shape, F32, kind="ExternalOutput").ap())
    gnn_resnorm_kernel(nc, *args)
    r = run_bass_kernel_spmd(nc, [arrays], core_ids=[0])
    return r.results[0]["out"]
```
